# Optimizing a Trainium2 kernel written in Bass

```python
import numpy as np
import jax
import jax.numpy as jnp

def _softmax(x, axis=-1):
    return jax.nn.softmax(x, axis=axis)

def _gelu(x):
    return jax.nn.gelu(x, approximate=True)

def _silu(x):
    return jax.nn.silu(x)

def _sigmoid(x):
    return jax.nn.sigmoid(x)

def _layernorm(x, axis=-1, eps=1e-05):
    m = jnp.mean(x, axis=axis, keepdims=True)
    v = jnp.var(x, axis=axis, keepdims=True)
    return (x - m) / jnp.sqrt(v + eps)

def _scatter_add(tgt, idx, src, axis=0):
    return tgt.at[idx].add(src)

def _segment_sum(src, seg, n):
    return jax.ops.segment_sum(src, seg, n)
kernel_name = 'mk_perceiver_d1_seqx_r4_095fae'

def setup_inputs(seed: int=0):
    np.random.seed(seed)
    _w = jnp.asarray

    def _rec_inputs():
        import jax
        import jax.numpy as jnp
        _rk = jax.random.key(seed)
        x = -0.0002928 + 1 * jax.random.normal(jax.random.fold_in(_rk, 1), (4, 256, 256), jnp.float32)
        _lenS = 256 - jax.random.randint(jax.random.fold_in(_rk, 7), (4,), 0, max(1, 256 // 4) + 1, jnp.int32)
        _lenS2 = 4096 - jax.random.randint(jax.random.fold_in(_rk, 8), (4,), 0, max(1, 4096 // 4) + 1, jnp.int32)
        _ctx_1024P = jax.random.normal(jax.random.fold_in(_rk, 11), (4, 16, 256), jnp.float32)
        _ctx_1024c = jax.random.dirichlet(jax.random.fold_in(_rk, 511), 0.3 * jnp.ones((16,), jnp.float32), (4, 4096))
        _ctx_1024t = jnp.einsum('bsk,bkd->bsd', _ctx_1024c, _ctx_1024P)
        _ctx_1024t = _ctx_1024t * jax.lax.rsqrt(jnp.mean(jnp.square(_ctx_1024t)) + 1e-12) * 0.953939
        ctx_1024 = -1.39393e-06 + 0.999914 * (_ctx_1024t + 0.3 * jax.random.normal(jax.random.fold_in(_rk, 611), (4, 4096, 256), jnp.float32))
        return (x, ctx_1024)
    x, ctx_1024 = _rec_inputs()

    def _L0_xattn_setup():
        import jax, jax.numpy as jnp
        import numpy as np
        D_MODEL = 256
        N_HEADS = 16
        D_HEAD = D_MODEL // N_HEADS
        key = jax.random.key(seed)
        ks = jax.random.split(key, 11)
        B, T = (2, 512)
        s = 1.0 / np.sqrt(D_MODEL)
        return {'query': jax.random.normal(ks[0], (B, T, D_MODEL), dtype=jnp.float32), 'key': jax.random.normal(ks[1], (B, T, D_MODEL), dtype=jnp.float32), 'value': jax.random.normal(ks[2], (B, T, D_MODEL), dtype=jnp.float32), 'Wq': jax.random.normal(ks[3], (D_MODEL, D_MODEL), dtype=jnp.float32) * s, 'bq': jnp.zeros((D_MODEL,), dtype=jnp.float32), 'Wk': jax.random.normal(ks[4], (D_MODEL, D_MODEL), dtype=jnp.float32) * s, 'bk': jnp.zeros((D_MODEL,), dtype=jnp.float32), 'Wv': jax.random.normal(ks[5], (D_MODEL, D_MODEL), dtype=jnp.float32) * s, 'bv': jnp.zeros((D_MODEL,), dtype=jnp.float32), 'Wh': jax.random.normal(ks[6], (D_MODEL, D_MODEL), dtype=jnp.float32) * s, 'bh': jnp.zeros((D_MODEL,), dtype=jnp.float32)}
    _L0_xattn_all = _L0_xattn_setup()
    _L0_xattn_in = {k: v for k, v in _L0_xattn_all.items() if k in ('Wq', 'bq', 'Wk', 'bk', 'Wv', 'bv', 'Wh', 'bh')}
    del _L0_xattn_all

    def _L0_attn_setup():
        import jax, jax.numpy as jnp
        import numpy as np
        EMBED = 256
        HEADS = 16
        HD = EMBED // HEADS
        M = 32
        R = 2
        EPS = 1e-06
        C_CONST = 2.0 + EPS
        CHUNK = 128

        def _features(x, omega, quad_nodes, quad_weights):
            B, H, T, D = x.shape
            xn = x / jnp.maximum(jnp.linalg.norm(x, axis=-1, keepdims=True), 1e-12)
            proj = jnp.einsum('bhtd,rhdm->rbhtm', xn, omega)
            s = quad_nodes[:, None, None, None, None]
            sqrt_2s = jnp.sqrt(2.0 * jnp.maximum(s, 0.0))
            arg = jnp.clip(proj * sqrt_2s - s, -20.0, 20.0)
            feat = jnp.exp(arg) / np.sqrt(M).astype(np.float32)
            feat = feat * jnp.sqrt(jnp.maximum(quad_weights, 0.0))[:, None, None, None, None]
            return jnp.transpose(feat, (1, 2, 3, 0, 4)).reshape(B, H, T, R * M)
        key = jax.random.key(seed)
        ks = jax.random.split(key, 4)
        B, T = (2, 512)
        x = jax.random.normal(ks[0], (B, T, EMBED), jnp.float32)
        Wqkv = jax.random.normal(ks[1], (EMBED, 3 * EMBED), jnp.float32) * 0.02
        bqkv = jnp.zeros((3 * EMBED,), jnp.float32)
        Wout = jax.random.normal(ks[2], (EMBED, EMBED), jnp.float32) * 0.02
        bout = jnp.zeros((EMBED,), jnp.float32)
        omega = jax.random.normal(ks[3], (R, HEADS, HD, M), jnp.float32)
        nodes, weights = np.polynomial.laguerre.laggauss(R)
        quad_nodes = jnp.asarray(nodes / C_CONST, jnp.float32)
        quad_weights = jnp.asarray(weights * (C_CONST / 4.0), jnp.float32)
        return {'x': x, 'Wqkv': Wqkv, 'bqkv': bqkv, 'Wout': Wout, 'bout': bout, 'omega': omega, 'quad_nodes': quad_nodes, 'quad_weights': quad_weights}
    _L0_attn_all = _L0_attn_setup()
    _L0_attn_in = {k: v for k, v in _L0_attn_all.items() if k in ('Wqkv', 'bqkv', 'Wout', 'bout', 'omega', 'quad_nodes', 'quad_weights')}
    del _L0_attn_all

    def _L0_ffn_setup():
        import jax, jax.numpy as jnp
        import numpy as np
        DIM = 256
        HIDDEN = 768
        SCALE = 1.0 / 127.0

        def _dequant(w_int, dtype):
            return w_int.astype(dtype) * jnp.asarray(SCALE, dtype)
        key = jax.random.key(seed)
        k_x, k_g, k_u, k_d = jax.random.split(key, 4)
        x = jax.random.normal(k_x, (4, 512, DIM), dtype=jnp.float32)
        w_gate = jax.random.randint(k_g, (HIDDEN, DIM), -127, 128, dtype=jnp.int32)
        w_up = jax.random.randint(k_u, (HIDDEN, DIM), -127, 128, dtype=jnp.int32)
        w_down = jax.random.randint(k_d, (DIM, HIDDEN), -127, 128, dtype=jnp.int32)
        return {'x': x, 'w_gate': w_gate, 'w_up': w_up, 'w_down': w_down}
    _L0_ffn_all = _L0_ffn_setup()
    _L0_ffn_in = {k: v for k, v in _L0_ffn_all.items() if k in ('w_gate', 'w_up', 'w_down')}
    del _L0_ffn_all
    return {'x': x, 'ctx_1024': ctx_1024, 'L0_xattn_Wq': _L0_xattn_in['Wq'], 'L0_xattn_bq': _L0_xattn_in['bq'], 'L0_xattn_Wk': _L0_xattn_in['Wk'], 'L0_xattn_bk': _L0_xattn_in['bk'], 'L0_xattn_Wv': _L0_xattn_in['Wv'], 'L0_xattn_bv': _L0_xattn_in['bv'], 'L0_xattn_Wh': _L0_xattn_in['Wh'], 'L0_xattn_bh': _L0_xattn_in['bh'], 'L0_attn_Wqkv': _L0_attn_in['Wqkv'], 'L0_attn_bqkv': _L0_attn_in['bqkv'], 'L0_attn_Wout': _L0_attn_in['Wout'], 'L0_attn_bout': _L0_attn_in['bout'], 'L0_attn_omega': _L0_attn_in['omega'], 'L0_attn_quad_nodes': _L0_attn_in['quad_nodes'], 'L0_attn_quad_weights': _L0_attn_in['quad_weights'], 'L0_ffn_w_gate': _L0_ffn_in['w_gate'], 'L0_ffn_w_up': _L0_ffn_in['w_up'], 'L0_ffn_w_down': _L0_ffn_in['w_down']}

def reference(x, ctx_1024, L0_xattn_Wq, L0_xattn_bq, L0_xattn_Wk, L0_xattn_bk, L0_xattn_Wv, L0_xattn_bv, L0_xattn_Wh, L0_xattn_bh, L0_attn_Wqkv, L0_attn_bqkv, L0_attn_Wout, L0_attn_bout, L0_attn_omega, L0_attn_quad_nodes, L0_attn_quad_weights, L0_ffn_w_gate, L0_ffn_w_up, L0_ffn_w_down):
    import jax
    import jax.numpy as jnp

    def _L0_xattn_ref(query, key, value, Wq, bq, Wk, bk, Wv, bv, Wh, bh):
        import jax, jax.numpy as jnp
        import numpy as np
        D_MODEL = 256
        N_HEADS = 16
        D_HEAD = D_MODEL // N_HEADS
        B, T_src, _ = query.shape
        T_dst = key.shape[1]
        Q = query @ Wq.T + bq
        K = key @ Wk.T + bk
        V = value @ Wv.T + bv
        Q = Q.reshape(B, T_src, N_HEADS, D_HEAD).transpose(0, 2, 1, 3)
        K = K.reshape(B, T_dst, N_HEADS, D_HEAD).transpose(0, 2, 1, 3)
        V = V.reshape(B, T_dst, N_HEADS, D_HEAD).transpose(0, 2, 1, 3)
        dot = jnp.einsum('bhsd,bhtd->bhst', Q, K) / np.sqrt(D_HEAD)
        scores = jax.nn.softmax(dot, axis=-1)
        out = jnp.einsum('bhst,bhtd->bhsd', scores, V)
        out = out.reshape(B, T_src, D_MODEL)
        return out @ Wh.T + bh

    def _L0_attn_ref(x, Wqkv, bqkv, Wout, bout, omega, quad_nodes, quad_weights):
        import jax, jax.numpy as jnp
        import numpy as np
        EMBED = 256
        HEADS = 16
        HD = EMBED // HEADS
        M = 32
        R = 2
        EPS = 1e-06
        C_CONST = 2.0 + EPS
        CHUNK = 128

        def _features(x, omega, quad_nodes, quad_weights):
            B, H, T, D = x.shape
            xn = x / jnp.maximum(jnp.linalg.norm(x, axis=-1, keepdims=True), 1e-12)
            proj = jnp.einsum('bhtd,rhdm->rbhtm', xn, omega)
            s = quad_nodes[:, None, None, None, None]
            sqrt_2s = jnp.sqrt(2.0 * jnp.maximum(s, 0.0))
            arg = jnp.clip(proj * sqrt_2s - s, -20.0, 20.0)
            feat = jnp.exp(arg) / np.sqrt(M).astype(np.float32)
            feat = feat * jnp.sqrt(jnp.maximum(quad_weights, 0.0))[:, None, None, None, None]
            return jnp.transpose(feat, (1, 2, 3, 0, 4)).reshape(B, H, T, R * M)
        B, T, C = x.shape
        qkv = x @ Wqkv + bqkv
        q, k, v = jnp.split(qkv, 3, axis=-1)
        resh = lambda t: t.reshape(B, T, HEADS, HD).transpose(0, 2, 1, 3)
        q, k, v = (resh(q), resh(k), resh(v))
        qf = _features(q, omega, quad_nodes, quad_weights)
        kf = _features(k, omega, quad_nodes, quad_weights)
        Fd = R * M
        nc = T // CHUNK
        to_chunks = lambda t, last: t.reshape(B, HEADS, nc, CHUNK, last).transpose(2, 0, 1, 3, 4)
        qc = to_chunks(qf, Fd)
        kc = to_chunks(kf, Fd)
        vc = to_chunks(v, HD)

        def step(carry, inp):
            kv_state, k_state = carry
            q_ch, k_ch, v_ch = inp
            kv_prod = jnp.einsum('bhtf,bhtd->bhtfd', k_ch, v_ch)
            kv_cur = jnp.cumsum(kv_prod, axis=2) + kv_state[:, :, None]
            k_cur = jnp.cumsum(k_ch, axis=2) + k_state[:, :, None]
            ctx = jnp.einsum('bhtf,bhtfd->bhtd', q_ch, kv_cur)
            den = jnp.maximum(jnp.einsum('bhtf,bhtf->bht', q_ch, k_cur), 1e-06)
            out_ch = ctx / den[..., None]
            return ((kv_cur[:, :, -1], k_cur[:, :, -1]), out_ch)
        init = (jnp.zeros((B, HEADS, Fd, HD), jnp.float32), jnp.zeros((B, HEADS, Fd), jnp.float32))
        _, outs = jax.lax.scan(step, init, (qc, kc, vc))
        out = outs.transpose(1, 2, 0, 3, 4).reshape(B, HEADS, T, HD)
        out = out.transpose(0, 2, 1, 3).reshape(B, T, C)
        return out @ Wout + bout

    def _L0_ffn_ref(x, w_gate, w_up, w_down):
        import jax, jax.numpy as jnp
        import numpy as np
        DIM = 256
        HIDDEN = 768
        SCALE = 1.0 / 127.0

        def _dequant(w_int, dtype):
            return w_int.astype(dtype) * jnp.asarray(SCALE, dtype)
        wg = _dequant(w_gate, x.dtype)
        wu = _dequant(w_up, x.dtype)
        wd = _dequant(w_down, x.dtype)
        gate = jnp.einsum('bsd,hd->bsh', x, wg)
        up = jnp.einsum('bsd,hd->bsh', x, wu)
        h = jax.nn.silu(gate) * up
        return jnp.einsum('bsh,dh->bsd', h, wd)
    x = x + _L0_xattn_ref(_layernorm(x, axis=-1), ctx_1024, ctx_1024, L0_xattn_Wq, L0_xattn_bq, L0_xattn_Wk, L0_xattn_bk, L0_xattn_Wv, L0_xattn_bv, L0_xattn_Wh, L0_xattn_bh)
    x = x + _L0_attn_ref(_layernorm(x, axis=-1), L0_attn_Wqkv, L0_attn_bqkv, L0_attn_Wout, L0_attn_bout, L0_attn_omega, L0_attn_quad_nodes, L0_attn_quad_weights)
    x = x + _L0_ffn_ref(_layernorm(x, axis=-1), L0_ffn_w_gate, L0_ffn_w_up, L0_ffn_w_down)
    return x

_drawn_inputs = setup_inputs


def setup_inputs(seed=0):
    import zlib

    import numpy as np

    out = dict(_drawn_inputs(seed))
    spreads = {'L0_xattn_bq': (0.0, 0.284),
     'L0_xattn_bk': (0.0, 0.8),
     'L0_xattn_bv': (0.0, 0.1),
     'L0_xattn_bh': (0.0, 0.1),
     'L0_attn_bqkv': (0.0, 0.1),
     'L0_attn_bout': (0.0, 0.1)}
    factors = {'L0_attn_omega': 8.0, 'L0_attn_quad_nodes': 4.231, 'L0_attn_quad_weights': 5.546}
    for name, (base, spread) in spreads.items():
        noise = np.random.default_rng([zlib.crc32(name.encode()), seed]).standard_normal(out[name].shape)
        drawn = base * np.exp(spread * noise) if base else spread * noise
        out[name] = jnp.asarray(drawn.astype(out[name].dtype))
    for name, factor in factors.items():
        out[name] = (out[name] * factor).astype(out[name].dtype)
    return out
```

```python
import concourse.bass as bass
from concourse import mybir
from contextlib import ExitStack

FP32 = mybir.dt.float32
FP32R = mybir.dt.float32r
BF16 = mybir.dt.bfloat16
INT32 = mybir.dt.int32
ALU = mybir.AluOpType
ACT = mybir.ActivationFunctionType
AX = mybir.AxisListType

B, S, D = 4, 256, 256
T = 4096
H = 16
DH = D // H
P = 128
CI = D // P
ST = S // P
CH = 512
NCH = T // CH
TT = CH // P
GH = 4
G = H // GH
STEPS = TT * G
M, R = 32, 2
F = R * M
HID = 768
HB = HID // P
EPS = 1e-5
QUANT = 1.0 / 127.0
KEY_PART = (0, 0, 0, 1, 1, 2)
QUERY_PART = (0, 1, 2, 0, 1, 0)
SLOTS = len(KEY_PART)
STACK = SLOTS * DH

LAG = 2
NPROB = 4

UNITS = {0: ("k", 0, 0), 1: ("k", 0, 1), 3: ("k", 1, 0), 4: ("k", 1, 1),
         6: ("v", 0, 0), 8: ("v", 1, 0), 10: ("v", 2, 0), 12: ("v", 3, 0)}

PRODUCTS = (["ln0T", "q", "maxT", "oT", "yT", "wh", "ln1T", "qkv", "qkT", "feat0", "feat1"]
            + [x for g in range(G) for x in ([f"feat{p}" for p in (2 * g + 2, 2 * g + 3) if p < H // 2]
                                             + [f"A{g * GH + j}" for j in range(GH)] + [f"pv{g}"])]
            + ["oT2", "yT2", "wout", "ln2T"]
            + [f"gu{k}" for k in range(HB)] + ["down"])
OPERANDS = (["ln0", "ln0T", "q", "max", "maxT", "o", "y", "yT", "ln1", "ln1T", "qk", "qkT"]
            + ["arg0", "feat0", "arg1", "feat1"]
            + [x for g in range(G) for x in ([f"{n}{p}" for p in (2 * g + 2, 2 * g + 3) if p < H // 2
                                              for n in ("arg", "feat")]
                                             + [f"A{g * GH + j}" for j in range(GH)])] + ["o2", "y2", "yT2", "ln2", "ln2T"]
            + [f"h{k}" for k in range(HB)] + ["out"])


def perceiver(nc, x, ctxT, wqT, bq, wkT, bk, wvT, bv, whT, bh, wqkv, bqkv, wout, bout,
              omega, nodes, weights, wgT, wuT, wdT, out):
    ctx = ExitStack()
    with ctx:
        def sb(name, shape, dt=FP32):
            return ctx.enter_context(nc.sbuf_tensor(name, shape, dt))

        def sem(name):
            return ctx.enter_context(nc.semaphore(name))

        def scratch(name, shape, dt):
            return nc.dram_tensor(name, shape, dt, kind="Internal").ap()

        kscr = scratch("kscr", [2, 3, D, CH], BF16)
        qscr = scratch("qscr", [3, D, S], BF16)
        oscr = scratch("oscr", [H, S, DH], FP32)
        mscr = scratch("mscr", [3, H, S], BF16)

        wk = [sb("wk_hi", [P, CI, D], FP32R), sb("wk_lo", [P, CI, D], FP32R)]
        wv = [sb("wv_hi", [P, CI, D], FP32R), sb("wv_lo", [P, CI, D], FP32R)]
        wq_sb, wh_sb, wout_sb = sb("wq_sb", [P, CI, D]), sb("wh_sb", [P, CI, D]), sb("wout_sb", [P, CI, D])
        wqkv_sb = sb("wqkv_sb", [P, CI, 3 * D])
        wg_sb, wu_sb = sb("wg_sb", [P, CI, HID]), sb("wu_sb", [P, CI, HID])
        wd_sb = sb("wd_sb", [P, HB, D])
        om_sb = sb("om_sb", [P, H // 2, P])
        bq_sb, bk_sb = sb("bq_sb", [P, CI]), sb("bk_sb", [P, CI])
        bv_sb, bh_sb, bout_sb = sb("bv_sb", [P, D]), sb("bh_sb", [P, D]), sb("bout_sb", [P, D])
        bqkv_sb = sb("bqkv_sb", [P, 3 * D])
        bqkv2 = sb("bqkv2", [P, ST, D])
        node, weight = sb("node", [P, 1]), sb("weight", [P, 1])
        node_neg, node_amp = sb("node_neg", [P, 1]), sb("node_amp", [P, 1])
        half_mask = sb("half_mask", [P, 2])
        half_power, root_power = sb("half_power", [P, ST, 2 * H]), sb("root_power", [P, 1])
        ident = sb("ident", [P, P])
        causal = sb("causal", [P, 3 * P])

        ctx_raw = [sb(f"ctx_raw{i}", [P, CI, CH]) for i in range(2)]
        ctx_hi = [sb(f"ctx_hi{i}", [P, CI, CH], FP32R) for i in range(2)]
        ctx_lo = [sb(f"ctx_lo{i}", [P, CI, CH], FP32R) for i in range(2)]
        kparts = sb("kparts", [P, 3, CI, CH], BF16)
        krest = sb("krest", [P, CH])
        kstack = [sb(f"kstack{i}", [P, H, CH], BF16) for i in range(2)]
        qparts = sb("qparts", [P, 3, CI, S], BF16)
        qstack = sb("qstack", [P, H, S], BF16)
        values = [sb(f"values{i}", [P, TT, H, 32]) for i in range(2)]
        probs = [sb(f"probs{i}", [P, GH * S]) for i in range(NPROB)]
        chunk_max = sb("chunk_max", [P, ST, H, NCH])
        neg_max = sb("neg_max", [P, ST, H])
        mrest, mparts = sb("mrest", [H, S]), sb("mparts", [H, 3, S], BF16)

        xs, xn = sb("xs", [P, ST, D]), sb("xn", [P, ST, D])
        xT = sb("xT", [P, CI, S])
        stats, mv = sb("stats", [P, ST, 6]), sb("mv", [P, ST, 2])
        veps, rstd = sb("veps", [P, ST]), sb("rstd", [P, ST])
        rden = sb("rden", [P, ST, H])
        y = sb("y", [P, ST, D])
        qrest = y
        qk = sb("qk", [P, ST, 2 * D])
        v1 = sb("v1", [P, ST, H, 32])
        o_sb = qk[:, :, :].rearrange("p t (g s) -> p (t g) s", s=S)
        ss, rnorm = sb("ss", [P, ST, 2 * H]), sb("rnorm", [P, ST, 2 * H])
        qkT = sb("qkT", [P, 4, S])
        feat = sb("feat", [P, 4, 2, S])
        kfeat = sb("kfeat", [P, 4, 2, S])
        amat = sb("amat", [P, GH, 3 * P])
        hid = feat[:, :, :, :].rearrange("p a b s -> p (a b) s")[:, 0:HB, :]
        gate_e = kfeat[:, 0, :, :]
        istage = amat[:, :, :].rearrange("p a b -> p (a b)")[:, 0:CI * HID].bitcast(INT32)
        wstage = feat[:, :, :, :].rearrange("p a b c -> p (a b c)")

        ps_s = [ctx.enter_context(nc.psum_tensor(f"ps_s{i}", [P, 1024], FP32)) for i in range(2)]
        ps_o = ctx.enter_context(nc.psum_tensor("ps_o", [P, 1024], FP32))
        ps_k = ctx.enter_context(nc.psum_tensor("ps_k", [P, 512], FP32))
        ps_v = ctx.enter_context(nc.psum_tensor("ps_v", [P, 512], FP32))
        bank = [ps_s[0][:, 0:512], ps_s[0][:, 512:1024], ps_s[1][:, 0:512], ps_s[1][:, 512:1024]]

        w_in, b_in, om_in, i_in, w_used = (sem(n) for n in ("w_in", "b_in", "om_in", "i_in", "w_used"))
        setup_dve, setup_pool = sem("setup_dve"), sem("setup_pool")
        ctx_in = [sem("ctx_in0"), sem("ctx_in1")]
        ctx_split = sem("ctx_split")
        k_proj, v_proj = sem("k_proj"), sem("v_proj")
        k_parts, v_ready = sem("k_parts"), sem("v_ready")
        k_written = sem("k_written")
        k_stacked = [sem("k_stacked0"), sem("k_stacked1")]
        scores, exp_done, pv_done = sem("scores"), sem("exp_done"), sem("pv_done")
        mscores, mreduced = sem("mscores"), sem("mreduced")
        product, operand = sem("product"), sem("operand")
        acted, powered, variance = sem("acted"), sem("powered"), sem("variance")
        x_in, q_written, q_stacked, m_written, m_stacked, o_written, o_in, stored = (
            sem(n) for n in ("x_in", "q_written", "q_stacked", "m_written", "m_stacked", "o_written", "o_in",
                             "stored"))

        block = ctx.enter_context(nc.Block())

        PPB = 2 * NCH
        NP, NA = len(PRODUCTS), len(OPERANDS)

        def prod(b, name):
            return NP * b + PRODUCTS.index(name) + 1

        def oper(b, name):
            return NA * b + OPERANDS.index(name) + 1

        def passes(eng, body):
            def run(attend, p0):
                body(p0, 0, p0 // 2, attend, True, False)
                with eng.Fori(0, NCH // 2 - 1) as c:
                    body(c * 2 + (p0 + 1), 1, c + p0 // 2, attend, False, False)
                    body(c * 2 + (p0 + 2), 0, c + (p0 // 2 + 1), attend, False, False)
                body(p0 + NCH - 1, 1, p0 // 2 + NCH // 2 - 1, attend, False, True)
            return run

        @block.sync
        def _(sp):
            def load_ctx(q, par, free=None):
                b, t0 = (q // PPB) % B, (q % NCH) * CH
                if free is not None:
                    b, t0 = sp.snap(b), sp.snap(t0)
                src = ctxT.rearrange("b (i p) t -> p b i t", p=P)
                if free is not None:
                    sp.wait_ge(ctx_split, free)
                sp.dma_start(ctx_raw[par][:, :, :],
                             src[:, bass.ds(b, 1), :, bass.ds(t0, CH)].rearrange("p b i t -> p (b i) t")
                             ).then_inc(ctx_in[par], 16)

            def stack_keys(q, par):
                written = q * 48 + 48
                if not isinstance(q, int):
                    written = sp.to_reg(written)
                sp.wait_ge(k_parts, q * 2 + 3)
                for i in range(3):
                    sp.dma_start(kscr[par, i].rearrange("(j p) t -> p j t", p=P),
                                 kparts[:, i, :, :]).then_inc(k_written, 16)
                sp.wait_ge(k_written, written)

            def stack_read(q, par):
                for n in range(SLOTS):
                    sp.dma_start(kstack[par][n * DH:(n + 1) * DH, :, :],
                                 kscr[par, KEY_PART[n]].rearrange("(h d) t -> d h t", d=DH)
                                 ).then_inc(k_stacked[par], 16)

            sp.sem_inc(stored, 16)
            wr = lambda a: a.rearrange("(i p) n -> p i n", p=P)
            sp.dma_start(wstage[:, 0:CI * D].rearrange("p (i n) -> p i n", i=CI), wr(wkT)).then_inc(w_in, 16)
            sp.dma_start(wstage[:, CI * D:2 * CI * D].rearrange("p (i n) -> p i n", i=CI), wr(wvT)).then_inc(w_in, 16)
            load_ctx(0, 0)
            load_ctx(1, 1)
            for dst, src in ((wq_sb, wqT), (wh_sb, whT), (wout_sb, wout), (wqkv_sb, wqkv)):
                sp.dma_start(dst[:, :, :], wr(src)).then_inc(b_in, 16)
            for dst, src in ((bq_sb, bq), (bk_sb, bk)):
                sp.dma_start(dst[:, :], src).then_inc(b_in, 16)
            for dst, src in ((bv_sb, bv), (bh_sb, bh), (bout_sb, bout), (bqkv_sb, bqkv)):
                sp.dma_start(dst[:, :], src.partition_broadcast(P)).then_inc(b_in, 16)
            for k in range(2 * R):
                r = k % R
                sp.dma_start(node[k * M:(k + 1) * M, :], nodes[r:r + 1].partition_broadcast(M)).then_inc(b_in, 16)
                sp.dma_start(weight[k * M:(k + 1) * M, :], weights[r:r + 1].partition_broadcast(M)).then_inc(b_in, 16)
            sp.wait_ge(setup_pool, 4)
            for h in range(H):
                row, col = (h % 8) * DH, (h % 2) * F
                sp.dma_start(om_sb[row:row + DH, h // 2, col:col + F],
                             omega[h * DH:(h + 1) * DH, :]).then_inc(om_in, 16)
            for n, (src, k) in enumerate(((wgT, CI), (wuT, CI), (wdT, HB))):
                if n:
                    sp.wait_ge(w_used, n)
                sp.dma_start(istage.rearrange("p (i n) -> p i n", i=k), wr(src)).then_inc(i_in, 16)

            stack_keys(0, 0)
            sp.wait_ge(setup_dve, 1)
            stack_read(0, 0)

            with sp.Fori(0, B) as b:
                sp.wait_ge(stored, b * 16 + 16)
                sp.dma_start(xs[:, :, :],
                             x[bass.ds(b, 1), :, :].rearrange("b (i p) d -> p (b i) d", p=P)).then_inc(x_in, 16)
                sp.wait_ge(operand, oper(b, "q"))
                for i in range(3):
                    sp.dma_start(qscr[i].rearrange("(j p) s -> p j s", p=P), qparts[:, i, :, :]).then_inc(q_written, 16)
                sp.wait_ge(q_written, b * 48 + 48)
                for n in range(SLOTS):
                    sp.dma_start(qstack[n * DH:(n + 1) * DH, :, :],
                                 qscr[QUERY_PART[n]].rearrange("(h d) s -> d h s", d=DH)).then_inc(q_stacked, 16)

                def body(p, par, half, attend, first, last):
                    q = b * PPB + p
                    load_ctx(q + 2, par, free=q + 1)
                    steps = b * (NCH * STEPS)
                    if attend and first:
                        used, count = mscores, steps + NCH * STEPS
                    elif attend:
                        used, count = scores, steps + (p - NCH) * STEPS
                    elif first:
                        used, count = exp_done, steps + 2
                    else:
                        used, count = mscores, steps + p * STEPS
                    count = sp.to_reg(count)
                    stack_keys(q + 1, 1 - par)
                    sp.wait_ge(used, count)
                    stack_read(q + 1, 1 - par)

                run = passes(sp, body)
                run(False, 0)
                sp.wait_ge(operand, oper(b, "maxT"))
                for i in range(3):
                    sp.dma_start(mscr[i], mparts[:, i, :]).then_inc(m_written, 16)
                sp.wait_ge(m_written, b * 48 + 48)
                for i in range(3):
                    sp.dma_start(qstack[STACK + i:STACK + i + 1, :, :],
                                 mscr[i:i + 1]).then_inc(m_stacked, 16)
                run(True, NCH)
                sp.wait_ge(operand, oper(b, "y"))
                for t in range(ST):
                    sp.dma_start(oscr[:, t * P:(t + 1) * P, :].rearrange("h s d -> s h d"),
                                 y[:, t, :].rearrange("p (h d) -> p h d", h=H)).then_inc(o_written, 16)
                sp.wait_ge(o_written, b * 32 + 32)
                sp.dma_start(y[:, :, :], oscr.rearrange("(t a) (u s) d -> (a u) t (s d)", t=ST, u=S // DH)
                             ).then_inc(o_in, 16)
                sp.wait_ge(operand, oper(b, "out"))
                sp.dma_start(out[bass.ds(b, 1), :, :].rearrange("b (i p) d -> p (b i) d", p=P),
                             xn[:, :, :]).then_inc(stored, 16)
            sp.wait_ge(stored, B * 16 + 16)
            sp.wait_ge(k_stacked[0], (B * PPB // 2 + 1) * 96)
            sp.wait_ge(k_stacked[1], (B * PPB // 2) * 96)
            sp.wait_ge(ctx_in[0], (B * PPB // 2 + 1) * 16)
            sp.wait_ge(ctx_in[1], (B * PPB // 2 + 1) * 16)

        @block.tensor
        def _(pe):
            mm = nc.tensor.matmul

            def project(unit, q, par):
                kind, j, part = unit
                hi, lo = ctx_hi[par], ctx_lo[par]
                if kind == "k":
                    if part == 0:
                        pe.wait_ge(k_parts, q * 2 + (j + 1))
                        if j == 0:
                            pe.wait_ge(ctx_split, q + 1)
                    for n, (w, c) in enumerate(((wk[0], hi), (wk[1], hi), (wk[0], lo))):
                        k = part
                        last = mm(ps_k[:, :], w[:, k, j * P:(j + 1) * P], c[:, k, :],
                                  start=(k == 0 and n == 0), stop=(k == CI - 1 and n == 2))
                    if part == CI - 1:
                        last.then_inc(k_proj, 1)
                else:
                    dst = ps_v[:, 0:D]
                    for k in range(CI):
                        for n, (c, w) in enumerate(((hi, wv[0]), (lo, wv[0]), (hi, wv[1]))):
                            last = mm(dst, c[:, k, j * P:(j + 1) * P], w[:, k, :],
                                      start=(k == 0 and n == 0), stop=(k == CI - 1 and n == 2))
                    last.then_inc(v_proj, 1)

            def transpose_blocks(dst, src):
                for i in range(CI):
                    for s in range(ST):
                        last = nc.tensor.transpose(dst[:, i * S + s * P:i * S + (s + 1) * P],
                                                   src[:, s, i * P:(i + 1) * P], ident[:, :])
                return last

            pe.sem_inc(pv_done, NPROB)
            pe.wait_ge(setup_dve, 2)
            pe.wait_ge(setup_pool, 4)
            pe.wait_ge(b_in, 16 * 18)
            for u in ((0, 0), (0, 1), (1, 0), (1, 1)):
                project(("k",) + u, 0, 0)

            with pe.Fori(0, B) as b:
                pe.wait_ge(operand, oper(b, "ln0"))
                transpose_blocks(bank[0], xn).then_inc(product, 1)
                pe.wait_ge(operand, oper(b, "ln0T"))
                for j in range(CI):
                    for k in range(CI):
                        last = mm(bank[1][:, j * S:(j + 1) * S], wq_sb[:, k, j * P:(j + 1) * P], xT[:, k, :],
                                  start=k == 0, stop=k == CI - 1)
                last.then_inc(product, 1)
                pe.wait_ge(operand, oper(b, "q"))
                pe.wait_ge(q_stacked, b * (16 * SLOTS) + 16 * SLOTS)

                def value_product(n, c, s, par, first, last_chunk, vtile):
                    i, g = s // G, s % G
                    pe.wait_ge(exp_done, n + 3)
                    if g == 0:
                        pe.wait_ge(v_ready, vtile + 2)
                    for j in range(GH):
                        last = mm(ps_o[32 * j:32 * j + 32, g * S:(g + 1) * S],
                                  values[par][:, i, g * GH + j, :], probs[s % NPROB][:, j * S:(j + 1) * S],
                                  start=bool(first and i == 0 and g % 2 == 0),
                                  stop=bool(last_chunk and i == TT - 1), skip_group_check=True)
                    last.then_inc(pv_done, 1)

                def body(p, par, half, attend, first, last_chunk):
                    q = b * PPB + p
                    count = b * (PPB // 2) + half
                    pe.wait_ge(k_stacked[par], count * 96 + 96)
                    if attend:
                        n0 = b * (NCH * STEPS) + (p - NCH) * STEPS
                        vt = b * (NCH * TT) + (p - NCH) * TT
                    else:
                        n0 = b * (NCH * STEPS) + p * STEPS
                    for s in range(STEPS):
                        if attend:
                            i, g = s // G, s % G
                            pe.wait_ge(exp_done, n0 + (s + 1))
                            for j in range(GH):
                                last = mm(ps_s[s % 2][:, j * S:(j + 1) * S],
                                          kstack[par][:, g * GH + j, i * P:(i + 1) * P],
                                          qstack[:, g * GH + j, :], start=True, stop=True)
                            last.then_inc(scores, 1)
                            if s >= LAG:
                                value_product(n0 + (s - LAG), p, s - LAG, par, first, last_chunk, vt + (s - LAG) // G)
                            elif not first:
                                value_product(n0 + (s - LAG), p, STEPS + s - LAG, 1 - par, False, False,
                                              vt + (-1))
                        else:
                            t, hp = s // (H // 2), s % (H // 2)
                            pe.wait_ge(mreduced, n0 + (s + 1))
                            for j in range(2):
                                h = 2 * hp + j
                                last = mm(ps_s[s % 2][:, j * CH:(j + 1) * CH],
                                          qstack[0:STACK, h, t * P:(t + 1) * P], kstack[par][0:STACK, h, :],
                                          start=True, stop=True)
                            last.then_inc(mscores, 1)
                        if s in UNITS:
                            wants = attend != last_chunk
                            if UNITS[s][0] == "k" or wants:
                                if UNITS[s][0] == "v":
                                    tile = UNITS[s][1]
                                    idx = (vt + TT if attend else b * (NCH * TT)) + tile
                                    pe.wait_ge(v_ready, idx + 1)
                                project(UNITS[s], q + 1, 1 - par)
                    if attend and last_chunk:
                        for s in range(STEPS - LAG, STEPS):
                            value_product(n0 + s, p, s, par, False, True, vt + s // G)

                run = passes(pe, body)
                run(False, 0)
                pe.wait_ge(operand, oper(b, "max"))
                for t in range(ST):
                    last = nc.tensor.transpose(bank[0][0:H, t * P:(t + 1) * P], neg_max[:, t, :], ident[:, :])
                last.then_inc(product, 1)
                pe.wait_ge(operand, oper(b, "maxT"))
                pe.wait_ge(m_stacked, b * 48 + 48)
                run(True, NCH)

                def back_to_rows(name):
                    pe.wait_ge(operand, oper(b, name))
                    for t in range(ST):
                        for g in range(G):
                            last = nc.tensor.transpose(ps_s[0][:, (t * G + g) * P:(t * G + g + 1) * P],
                                                       o_sb[:, g, t * P:(t + 1) * P], ident[:, :])
                    last.then_inc(product, 1)

                def project_rows(dst, w, n, last_k=CI):
                    for t in range(ST):
                        for k in range(CI):
                            last = mm(dst(t), xT[:, k, t * P:(t + 1) * P], w(k), start=k == 0, stop=k == CI - 1)
                    return last

                back_to_rows("o")
                pe.wait_ge(o_in, b * 16 + 16)
                transpose_blocks(bank[2], y).then_inc(product, 1)
                pe.wait_ge(operand, oper(b, "yT"))
                project_rows(lambda t: bank[3][:, t * D:(t + 1) * D], lambda k: wh_sb[:, k, :], D).then_inc(product, 1)
                pe.wait_ge(operand, oper(b, "ln1"))
                transpose_blocks(bank[0], xn).then_inc(product, 1)
                pe.wait_ge(operand, oper(b, "ln1T"))
                project_rows(lambda t: bank[2 + t], lambda k: wqkv_sb[:, k, 0:2 * D], 2 * D)
                project_rows(lambda t: ps_o[:, t * D:(t + 1) * D], lambda k: wqkv_sb[:, k, 2 * D:3 * D], D
                             ).then_inc(product, 1)
                pe.wait_ge(operand, oper(b, "qk"))
                for n in range(4):
                    for t in range(ST):
                        last = nc.tensor.transpose(ps_s[0][:, n * S + t * P:n * S + (t + 1) * P],
                                                   qk[:, t, n * P:(n + 1) * P], ident[:, :])
                last.then_inc(product, 1)
                pe.wait_ge(operand, oper(b, "qkT"))

                def feature_args(p):
                    if p >= 2:
                        pe.wait_ge(operand, oper(b, f"arg{p - 2}"))
                    for n in range(2):
                        last = mm(bank[p % 2][:, n * S:(n + 1) * S], om_sb[:, p, :], qkT[:, 2 * n + p // 4, :],
                                  start=True, stop=True)
                    last.then_inc(product, 1)

                feature_args(0)
                feature_args(1)
                for g in range(G):
                    for p in (2 * g + 2, 2 * g + 3):
                        if p < H // 2:
                            feature_args(p)
                    for h in range(g * GH, (g + 1) * GH):
                        p = h // 2
                        pe.wait_ge(operand, oper(b, f"feat{p}"))
                        if h >= 2:
                            pe.wait_ge(operand, oper(b, f"A{h - 2}"))
                        a = bank[2 + h % 2]
                        mm(a[:, 0:S], kfeat[:, p % 4, h % 2, 0:P], feat[:, p % 4, 0, :], start=True, stop=True)
                        mm(a[:, S:S + P], kfeat[:, p % 4, h % 2, P:S], feat[:, p % 4, 0, P:S], start=True,
                           stop=True).then_inc(product, 1)
                    pe.wait_ge(operand, oper(b, f"A{g * GH + GH - 1}"))
                    for j in range(GH):
                        mm(ps_o[32 * j:32 * j + 32, g * S:(g + 1) * S], v1[:, 0, g * GH + j, :],
                           amat[:, j, 0:S], start=True, stop=False, skip_group_check=True)
                        last = mm(ps_o[32 * j:32 * j + 32, g * S + P:(g + 1) * S], v1[:, 1, g * GH + j, :],
                                  amat[:, j, S:S + P], start=False, stop=True, skip_group_check=True)
                    last.then_inc(product, 1)
                back_to_rows("o2")
                pe.wait_ge(operand, oper(b, "y2"))
                transpose_blocks(bank[2], y).then_inc(product, 1)
                pe.wait_ge(operand, oper(b, "yT2"))
                project_rows(lambda t: bank[3][:, t * D:(t + 1) * D], lambda k: wout_sb[:, k, :], D).then_inc(product, 1)
                pe.wait_ge(operand, oper(b, "ln2"))
                transpose_blocks(bank[0], xn).then_inc(product, 1)
                pe.wait_ge(operand, oper(b, "ln2T"))
                for k in range(HB):
                    if k >= 4:
                        pe.wait_ge(operand, oper(b, f"h{k - 4}"))
                    for n, w in enumerate((wg_sb, wu_sb)):
                        for c in range(CI):
                            last = mm(bank[k % 4][:, n * S:(n + 1) * S], w[:, c, k * P:(k + 1) * P], xT[:, c, :],
                                      start=c == 0, stop=c == CI - 1)
                    last.then_inc(product, 1)
                pe.wait_ge(operand, oper(b, f"h{HB - 1}"))
                for t in range(ST):
                    for k in range(HB):
                        last = mm(ps_o[:, t * D:(t + 1) * D], hid[:, k, t * P:(t + 1) * P], wd_sb[:, k, :],
                                  start=k == 0, stop=k == HB - 1)
                last.then_inc(product, 1)

        @block.gpsimd
        def _(pool):
            pool.memset(om_sb[:, :, :], 0.0).then_inc(setup_pool, 1)
            pool.memset(ident[:, :], 0.0)
            pool.memset(causal[:, :], 1.0)
            pool.memset(half_power[:, :, :], -0.5)
            pool.memset(root_power[:, :], 0.5).then_inc(setup_pool, 1)
            pool.drain()
            pool.affine_select(out=ident[:, :], in_=ident[:, :], compare_op=ALU.not_equal, fill=1.0,
                               base=0, pattern=[[-1, P]], channel_multiplier=1).then_inc(setup_pool, 1)
            for k in (0, 2):
                blk = causal[:, k * P:(k + 1) * P]
                last = pool.affine_select(out=blk, in_=blk, compare_op=ALU.is_ge, fill=0.0,
                                          base=0, pattern=[[1, P]], channel_multiplier=-1)
            last.then_inc(setup_pool, 1)
            pool.wait_ge(variance, 1)
            pool.tensor_tensor(node_amp[:, :], node_amp[:, :], root_power[:, :], ALU.pow).then_inc(powered, 1)
            with pool.Fori(0, B) as b:
                for k in range(4):
                    pool.wait_ge(variance, b * 4 + (k + 2))
                    if k == 2:
                        pool.tensor_tensor(rnorm[:, :, :], ss[:, :, :], half_power[:, :, :], ALU.pow).then_inc(powered, 1)
                    else:
                        pool.tensor_tensor(rstd[:, :], veps[:, :], half_power[:, :, 0], ALU.pow).then_inc(powered, 1)

        @block.scalar
        def _(act):
            act.sem_inc(exp_done, 2)
            with act.Fori(0, B) as b:
                with act.Fori(0, NCH) as c:
                    for s in range(STEPS):
                        n = b * (NCH * STEPS) + c * STEPS + s
                        act.wait_ge(scores, n + 1)
                        act.wait_ge(pv_done, n + 1)
                        nc.scalar.activation(probs[s % NPROB][:, :], ps_s[s % 2][:, :], ACT.Exp,
                                             scale=float(DH) ** -0.5).then_inc(exp_done, 1)
                for p in range(H // 2):
                    act.wait_ge(operand, oper(b, f"arg{p}"))
                    nc.scalar.activation(feat[:, p % 4, :, :], feat[:, p % 4, :, :], ACT.Exp).then_inc(acted, 1)
                for k in range(HB):
                    act.wait_ge(product, prod(b, f"gu{k}"))
                    if k >= 2:
                        act.wait_ge(operand, oper(b, f"h{k - 2}"))
                    nc.scalar.activation(gate_e[:, k % 2, :], bank[k % 4][:, 0:S], ACT.Exp, scale=-1.0
                                         ).then_inc(acted, 1)

        @block.vector
        def _(dve):
            v = nc.vector
            NACT = H // 2 + HB

            for i in range(2):
                v.memset(kstack[i][STACK:P, :, :], 1.0)
                v.memset(values[i][:, :, :, DH:32], 0.0)
            v.memset(qstack[STACK:P, :, :], 0.0)
            v.memset(v1[:, :, :, DH:32], 0.0)
            v.memset(half_mask[:, :], 0.0)
            dve.drain()
            for i in range(2):
                v.memset(values[i][:, :, :, DH:DH + 1], 1.0)
            v.memset(v1[:, :, :, DH:DH + 1], 1.0).then_inc(setup_dve, 1)
            dve.sem_inc(k_parts, 1)
            dve.sem_inc(v_ready, 1)
            dve.sem_inc(mreduced, 2)

            def cut(hi, lo, src):
                v.tensor_copy(hi, src)
                dve.drain()
                return v.tensor_tensor(lo, src, hi.bitcast(FP32), ALU.subtract)

            def split_ctx(q, par, count):
                dve.wait_ge(ctx_in[par], count * 16 + 16)
                cut(ctx_hi[par][:, :, :], ctx_lo[par][:, :, :], ctx_raw[par][:, :, :]).then_inc(ctx_split, 1)

            def keys_out(q, j):
                dve.wait_ge(k_proj, q * 2 + (j + 1))
                if j == 0:
                    dve.wait_ge(k_written, q * 48)
                bias = bk_sb[:, j:j + 1]
                v.tensor_scalar(kparts[:, 0, j, :], ps_k[:, :], bias, None, ALU.add)
                dve.drain()
                v.scalar_tensor_tensor(krest[:, :], ps_k[:, :], bias, kparts[:, 0, j, :], ALU.add, ALU.subtract)
                dve.drain()
                v.tensor_copy(kparts[:, 1, j, :], krest[:, :])
                dve.drain()
                v.tensor_tensor(kparts[:, 2, j, :], krest[:, :], kparts[:, 1, j, :], ALU.subtract
                                ).then_inc(k_parts, 1)

            def values_out(idx, tile, par, steps_before):
                dve.wait_ge(v_proj, idx + 1)
                if tile == 0:
                    dve.wait_ge(pv_done, steps_before + NPROB)
                v.tensor_tensor(values[par][:, tile, :, 0:DH],
                                ps_v[:, 0:D].rearrange("p (h d) -> p h d", h=H),
                                bv_sb[:, :].rearrange("p (h d) -> p h d", h=H), ALU.add).then_inc(v_ready, 1)

            dve.wait_ge(w_in, 32)
            for n, w in enumerate((wk, wv)):
                src = wstage[:, n * CI * D:(n + 1) * CI * D].rearrange("p (i n) -> p i n", i=CI)
                cut(w[0][:, :, :], w[1][:, :, :], src)
            dve.drain()
            dve.sem_inc(setup_dve, 1)
            dve.wait_ge(ctx_in[0], 16)
            cut(ctx_hi[0][:, :, :], ctx_lo[0][:, :, :], ctx_raw[0][:, :, :]).then_inc(ctx_split, 1)
            dve.wait_ge(ctx_in[1], 16)
            cut(ctx_hi[1][:, :, :], ctx_lo[1][:, :, :], ctx_raw[1][:, :, :]).then_inc(ctx_split, 1)
            dve.wait_ge(b_in, 16 * 18)
            for j in range(CI):
                dve.wait_ge(k_proj, j + 1)
                bias = bk_sb[:, j:j + 1]
                v.tensor_scalar(kparts[:, 0, j, :], ps_k[:, :], bias, None, ALU.add)
                dve.drain()
                v.scalar_tensor_tensor(krest[:, :], ps_k[:, :], bias, kparts[:, 0, j, :], ALU.add, ALU.subtract)
                dve.drain()
                v.tensor_copy(kparts[:, 1, j, :], krest[:, :])
                dve.drain()
                v.tensor_tensor(kparts[:, 2, j, :], krest[:, :], kparts[:, 1, j, :], ALU.subtract
                                ).then_inc(k_parts, 1)
            for t in range(ST):
                v.tensor_copy(bqkv2[:, t, :], bqkv_sb[:, 2 * D:3 * D])
            v.tensor_scalar(node_amp[:, :], node[:, :], 0.0, 2.0, ALU.max, ALU.mult).then_inc(variance, 1)
            v.tensor_scalar(node_neg[:, :], node[:, :], -1.0, None, ALU.mult)
            for k in range(2):
                v.tensor_scalar(half_mask[k * F:(k + 1) * F, k:k + 1], weight[k * F:(k + 1) * F, :],
                                0.0, 1.0 / M, ALU.max, ALU.mult)
            for n, (dst, k) in enumerate(((wg_sb, CI), (wu_sb, CI), (wd_sb, HB))):
                dve.wait_ge(i_in, 16 * n + 16)
                v.tensor_scalar(dst[:, :, :], istage.rearrange("p (i n) -> p i n", i=k), QUANT, None, ALU.mult
                                ).then_inc(w_used, 1)
            dve.wait_ge(om_in, 16 * H)
            dve.wait_ge(powered, 1)
            dve.wait_ge(setup_pool, 4)

            def layernorm(b, k, name):
                for t in range(ST):
                    v.bn_stats(stats[:, t, :], xs[:, t, :])
                dve.drain()
                for t in range(ST):
                    v.bn_aggr(mv[:, t, :], stats[:, t, :])
                dve.drain()
                v.tensor_scalar(veps[:, :], mv[:, :, 1], EPS, None, ALU.add).then_inc(variance, 1)
                dve.wait_ge(powered, b * 4 + (k + 2))
                for t in range(ST):
                    last = v.tensor_scalar(xn[:, t, :], xs[:, t, :], mv[:, t, 0:1], rstd[:, t:t + 1],
                                           ALU.subtract, ALU.mult)
                last.then_inc(operand, 1)

            def copy_out(b, src, name):
                dve.wait_ge(product, prod(b, name))
                v.tensor_copy(xT[:, :, :], src.rearrange("p (i s) -> p i s", i=CI)).then_inc(operand, 1)

            def bands_out(b, name):
                dve.wait_ge(product, prod(b, name))
                v.tensor_copy(o_sb[:, :, :], ps_o[:, :].rearrange("p (g s) -> p g s", g=G)).then_inc(operand, 1)

            def normalise(b, name, floor):
                dve.wait_ge(product, prod(b, name))
                heads = ps_s[0][:, :].rearrange("p (a c) -> p a c", c=32)
                flat = rden[:, :, :].rearrange("p t h -> p (t h)")
                if floor is None:
                    v.reciprocal(flat, heads[:, :, DH])
                else:
                    v.tensor_scalar(flat, heads[:, :, DH], floor, None, ALU.max)
                    dve.drain()
                    v.reciprocal(flat, flat)
                dve.drain()
                v.tensor_tensor(y[:, :, :].rearrange("p t (h d) -> p (t h) d", d=DH), heads[:, :, 0:DH],
                                flat.unsqueeze(2).to_broadcast([P, ST * H, DH]), ALU.mult).then_inc(operand, 1)

            def residual(b, name, src, bias):
                dve.wait_ge(product, prod(b, name))
                v.tensor_tensor(xs[:, :, :], xs[:, :, :], src.rearrange("p (t d) -> p t d", t=ST), ALU.add)
                dve.drain()
                v.tensor_tensor(xs[:, :, :], xs[:, :, :],
                                bias[:, :].unsqueeze(1).to_broadcast([P, ST, D]), ALU.add)
                dve.drain()

            with dve.Fori(0, B) as b:
                dve.wait_ge(x_in, b * 16 + 16)
                dve.wait_ge(stored, b * 16 + 16)
                layernorm(b, 0, "ln0")
                copy_out(b, bank[0], "ln0T")
                dve.wait_ge(product, prod(b, "q"))
                for j in range(CI):
                    src, bias = bank[1][:, j * S:(j + 1) * S], bq_sb[:, j:j + 1]
                    v.tensor_scalar(qparts[:, 0, j, :], src, bias, None, ALU.add)
                    dve.drain()
                    v.scalar_tensor_tensor(qrest[:, j, :], src, bias, qparts[:, 0, j, :], ALU.add, ALU.subtract)
                dve.drain()
                v.tensor_copy(qparts[:, 1, :, :], qrest[:, :, :])
                dve.drain()
                v.tensor_tensor(qparts[:, 2, :, :], qrest[:, :, :], qparts[:, 1, :, :], ALU.subtract
                                ).then_inc(operand, 1)

                def body(p, par, half, attend, first, last_chunk):
                    q = b * PPB + p
                    if attend:
                        keys_out(q + 1, 0)
                        keys_out(q + 1, 1)
                        if not last_chunk:
                            for tile in range(TT):
                                values_out(b * (NCH * TT) + (p - NCH + 1) * TT + tile, tile, 1 - par,
                                           b * (NCH * STEPS) + (p - NCH) * STEPS)
                    else:
                        n0 = b * (NCH * STEPS) + p * STEPS
                        for s in range(STEPS):
                            t, hp = s // (H // 2), s % (H // 2)
                            dve.wait_ge(mscores, n0 + (s + 1))
                            v.tensor_reduce(chunk_max[:, t, 2 * hp:2 * hp + 2, bass.ds(p, 1)],
                                            ps_s[s % 2][:, :].rearrange("p (h t) -> p h t", h=2), AX.X, ALU.max
                                            ).then_inc(mreduced, 1)
                            if s in UNITS:
                                kind, j, part = UNITS[s]
                                if kind == "k" and part == CI - 1:
                                    keys_out(q + 1, j)
                                if kind == "v" and last_chunk:
                                    values_out(b * (NCH * TT) + j, j, 1 - par, b * (NCH * STEPS))
                    split_ctx(q + 2, par, b * (PPB // 2) + half + 1)

                run = passes(dve, body)
                run(False, 0)
                dve.drain()
                v.tensor_reduce(neg_max[:, :, :], chunk_max[:, :, :, :], AX.X, ALU.max, negate=True
                                ).then_inc(operand, 1)
                dve.wait_ge(product, prod(b, "maxT"))
                src = bank[0][0:H, 0:S]
                v.tensor_copy(mparts[:, 0, :], src)
                dve.drain()
                v.tensor_tensor(mrest[:, :], src, mparts[:, 0, :], ALU.subtract)
                dve.drain()
                v.tensor_copy(mparts[:, 1, :], mrest[:, :])
                dve.drain()
                v.tensor_tensor(mparts[:, 2, :], mrest[:, :], mparts[:, 1, :], ALU.subtract).then_inc(operand, 1)
                run(True, NCH)

                dve.wait_ge(pv_done, b * (NCH * STEPS) + (NCH * STEPS + NPROB))
                v.tensor_copy(o_sb[:, :, :], ps_o[:, :].rearrange("p (g s) -> p g s", g=G)).then_inc(operand, 1)
                normalise(b, "oT", None)
                copy_out(b, bank[2], "yT")
                residual(b, "wh", bank[3], bh_sb)
                layernorm(b, 1, "ln1")
                copy_out(b, bank[0], "ln1T")
                dve.wait_ge(product, prod(b, "qkv"))
                for t in range(ST):
                    v.tensor_tensor(qk[:, t, :], bank[2 + t], bqkv_sb[:, 0:2 * D], ALU.add)
                v.tensor_tensor(v1[:, :, :, 0:DH].rearrange("p t h d -> p (t h) d"),
                                ps_o[:, 0:ST * D].rearrange("p (a d) -> p a d", d=DH),
                                bqkv2[:, :, :].rearrange("p t (h d) -> p (t h) d", d=DH), ALU.add)
                dve.drain()
                sq = feat[:, 0:2, :, :].rearrange("p a b s -> p (a b s)").rearrange("p (t n) -> p t n", t=ST)
                v.tensor_tensor(sq, qk[:, :, :], qk[:, :, :], ALU.mult)
                dve.drain()
                v.tensor_reduce(ss[:, :, :].rearrange("p t h -> p (t h)"),
                                sq.rearrange("p t (h d) -> p (t h) d", d=DH), AX.X, ALU.add)
                dve.drain()
                v.tensor_scalar(ss[:, :, :], ss[:, :, :], 1e-24, None, ALU.max).then_inc(variance, 1)
                dve.wait_ge(powered, b * 4 + 4)
                qk3 = qk[:, :, :].rearrange("p t (h d) -> p (t h) d", d=DH)
                v.tensor_tensor(qk3, qk3, rnorm[:, :, :].rearrange("p t h -> p (t h)").unsqueeze(2)
                                .to_broadcast([P, ST * 2 * H, DH]), ALU.mult).then_inc(operand, 1)
                dve.wait_ge(product, prod(b, "qkT"))
                v.tensor_copy(qkT[:, :, :], ps_s[0][:, :].rearrange("p (n s) -> p n s", n=4)).then_inc(operand, 1)
                def features(p):
                    dve.wait_ge(product, prod(b, f"feat{p}"))
                    if p >= 4:
                        dve.wait_ge(product, prod(b, f"pv{p // 2 - 2}"))
                    f = feat[:, p % 4, :, :].rearrange("p a s -> p (a s)")
                    v.tensor_scalar(f, bank[p % 2], node_amp[:, :], node_neg[:, :], ALU.mult, ALU.add)
                    dve.drain()
                    v.tensor_scalar(f, f, 20.0, -20.0, ALU.min, ALU.max).then_inc(operand, 1)
                    dve.wait_ge(acted, b * NACT + (p + 1))
                    for k in range(2):
                        last = v.tensor_scalar(kfeat[:, p % 4, k, :], feat[:, p % 4, 1, :], half_mask[:, k:k + 1],
                                               None, ALU.mult)
                    last.then_inc(operand, 1)

                features(0)
                features(1)
                for g in range(G):
                    for p in (2 * g + 2, 2 * g + 3):
                        if p < H // 2:
                            features(p)
                    for h in range(g * GH, (g + 1) * GH):
                        dve.wait_ge(product, prod(b, f"A{h}"))
                        if g and h % GH == 0:
                            dve.wait_ge(product, prod(b, f"pv{g - 1}"))
                        v.tensor_tensor(amat[:, h % GH, :], bank[2 + h % 2][:, 0:3 * P], causal[:, :], ALU.mult
                                        ).then_inc(operand, 1)
                bands_out(b, f"pv{G - 1}")
                normalise(b, "oT2", 1e-6)
                copy_out(b, bank[2], "yT2")
                residual(b, "wout", bank[3], bout_sb)
                layernorm(b, 3, "ln2")
                copy_out(b, bank[0], "ln2T")
                for k in range(HB):
                    dve.wait_ge(acted, b * NACT + (H // 2 + k + 1))
                    e = gate_e[:, k % 2, :]
                    v.tensor_scalar(e, e, 1.0, None, ALU.add)
                    dve.drain()
                    v.reciprocal(e, e)
                    dve.drain()
                    v.tensor_tensor(e, e, bank[k % 4][:, 0:S], ALU.mult)
                    dve.drain()
                    v.tensor_tensor(hid[:, k, :], e, bank[k % 4][:, S:2 * S], ALU.mult).then_inc(operand, 1)
                dve.wait_ge(product, prod(b, "down"))
                v.tensor_tensor(xn[:, :, :], xs[:, :, :],
                                ps_o[:, 0:ST * D].rearrange("p (t d) -> p t d", t=ST), ALU.add).then_inc(operand, 1)


def kernel(**inputs):
    import numpy as np
    import concourse.bacc as bacc
    from concourse.bass_utils import run_bass_kernel_spmd

    i = {k: np.asarray(a) for k, a in inputs.items()}
    omega = i["L0_attn_omega"]
    arrays = {
        "x": i["x"], "ctxT": i["ctx_1024"].transpose(0, 2, 1),
        "wqT": i["L0_xattn_Wq"].T, "bq": i["L0_xattn_bq"].reshape(CI, P).T, "wkT": i["L0_xattn_Wk"].T, "bk": i["L0_xattn_bk"].reshape(CI, P).T,
        "wvT": i["L0_xattn_Wv"].T, "bv": i["L0_xattn_bv"], "whT": i["L0_xattn_Wh"].T, "bh": i["L0_xattn_bh"],
        "wqkv": i["L0_attn_Wqkv"], "bqkv": i["L0_attn_bqkv"], "wout": i["L0_attn_Wout"], "bout": i["L0_attn_bout"],
        "omega": omega.transpose(1, 2, 0, 3).reshape(H * DH, F),
        "nodes": i["L0_attn_quad_nodes"], "weights": i["L0_attn_quad_weights"],
        "wgT": i["L0_ffn_w_gate"].T, "wuT": i["L0_ffn_w_up"].T, "wdT": i["L0_ffn_w_down"].T,
    }
    arrays = {k: np.ascontiguousarray(a) for k, a in arrays.items()}
    nc = bacc.Bacc("TRN2", target_bir_lowering=False, num_devices=1)
    aps = [nc.dram_tensor(k, a.shape, mybir.dt.from_np(a.dtype), kind="ExternalInput").ap()
           for k, a in arrays.items()]
    out = nc.dram_tensor("out", (B, S, D), FP32, kind="ExternalOutput").ap()
    perceiver(nc, *aps, out)
    r = run_bass_kernel_spmd(nc, [arrays], core_ids=[0])
    return r.results[0]["out"]
```

```python
import concourse.bass as bass
from concourse import mybir
from contextlib import ExitStack

FP32 = mybir.dt.float32
FP32R = mybir.dt.float32r
BF16 = mybir.dt.bfloat16
INT32 = mybir.dt.int32
ALU = mybir.AluOpType
ACT = mybir.ActivationFunctionType
AX = mybir.AxisListType

B, S, D = 4, 256, 256
T = 4096
H = 16
DH = D // H
P = 128
CI = D // P
ST = S // P
CH = 512
NCH = T // CH
TT = CH // P
GH = 4
G = H // GH
STEPS = TT * G
M, R = 32, 2
F = R * M
HID = 768
HB = HID // P
EPS = 1e-5
QUANT = 1.0 / 127.0
KEY_PART = (0, 0, 0, 1, 1, 2)
QUERY_PART = (0, 1, 2, 0, 1, 0)
SLOTS = len(KEY_PART)
STACK = SLOTS * DH

LAG = 2
NPROB = 4
SAMPLE = 64
DEN_LEAST, DEN_MOST = 2.0 ** -40, 2.0 ** 40

UNITS = {0: ("k", 0, 0), 1: ("k", 0, 1), 3: ("k", 1, 0), 4: ("k", 1, 1),
         6: ("v", 0, 0), 8: ("v", 1, 0), 10: ("v", 2, 0), 12: ("v", 3, 0)}

VECTOR_ONLY = ("ln0", "kbd", "qcopy", "qcopy0", "fullmax", "o")
HEAD = ["ln0", "ln0T", "q", "kbd", "max0", "max1", "max2", "max3", "maxT", "qcopy"]
HEAD_GENERAL = ["ln0", "ln0T", "q", "qcopy0", "fullmax", "maxT", "qcopy"]
TAIL = (["o", "oT0", "oT1", "yT", "wh", "ln1T", "qk0", "qk1", "v", "qkT0", "qkT1"]
        + [x for g in range(G) for x in ([f"feat{2 * g}", f"feat{2 * g + 1}"]
                                         + [f"A{g * GH + j}" for j in range(GH)] + [f"pv{g}"])]
        + ["o2T0", "o2T1", "y2T", "wout", "ln2T"] + [f"gu{k}" for k in range(HB)] + ["down"])
FEATS = [f"feat{p}" for p in range(H // 2)]
GATES = [f"gu{k}" for k in range(HB)]

AT = {"o": 0, "oT0": 3, "oT1": 5, "yT": 18, "wh": 20, "ln1T": 26, "qk0": 28, "qk1": 30, "v": 32,
      "qkT0": 37, "qkT1": 39}
for _g in range(G):
    for _k, _name in enumerate((f"feat{2 * _g}", f"feat{2 * _g + 1}")):
        AT[_name] = 41 + 8 * _g + _k
    for _j in range(GH):
        AT[f"A{_g * GH + _j}"] = 44 + 8 * _g + _j
    AT[f"pv{_g}"] = 48 + 8 * _g
AT.update({"o2T0": 75, "o2T1": 77, "y2T": 79, "wout": 81, "ln2T": 87, "down": 107})
for _k in range(HB):
    AT[f"gu{_k}"] = 89 + 3 * _k
HEAD_AT = {"ln0": 110, "ln0T": 113, "q": 115, "kbd": 118, "max0": 119, "max1": 120, "max2": 121, "max3": 122,
           "maxT": 123}
HEAD_AT_FIRST = {"ln0": 112, "ln0T": 115, "q": 117, "kbd": 119, "max0": 120, "max1": 121, "max2": 122,
                 "max3": 123, "maxT": 124}
ACT_BEHIND = {**{n: 2 for n in FEATS}, **{n: 1 for n in GATES}}


class Signals(dict):

    NAMES = ("ctx_in", "ctx_split",
             "k_proj", "v_proj",
             "k_parts", "v_ready",
             "k_written",
             "scores", "exp_done", "pv_done",
             "mscores", "mreduced",
             "x_in", "q_written", "q_stacked", "m_written", "m_stacked", "o_written", "o_in", "stored",
             "product", "operand",
             "variance", "powered",
             "args", "acted", "kfeat",
             "landed")

    def __init__(self, sem, prefix, head):
        for name in self.NAMES:
            self[name] = sem(prefix + name)
        self["k_stacked"] = [sem(prefix + "k_stacked0"), sem(prefix + "k_stacked1")]
        self.stages = {
            "product": ([n for n in head if n not in VECTOR_ONLY], [n for n in TAIL if n not in VECTOR_ONLY]),
            "operand": (head, TAIL),
            "powered": (["ln0"], ["wh", "v", "wout"]),
            "args": ([], FEATS), "acted": ([], FEATS + GATES), "kfeat": ([], FEATS),
            "x_in": (["x"], ["x"]),
        }

    def at(self, kind, clock, name):
        heads, tails, is_tail = clock
        per_head, per_tail = self.stages[kind]
        total = (per_tail if is_tail else per_head).index(name) + 1
        if per_head:
            total = heads * len(per_head) + total
        if per_tail:
            total = tails * len(per_tail) + total
        return total


def perceiver(nc, x, ctxT, wqT, bq, wkT, bk, wvT, bv, whT, bh, wqkv, bqkv, wout, bout,
              omega, nodes, weights, wgT, wuT, wdT, out):
    ctx = ExitStack()
    with ctx:
        def sb(name, shape, dt=FP32):
            return ctx.enter_context(nc.sbuf_tensor(name, shape, dt))

        def sem(name):
            return ctx.enter_context(nc.semaphore(name))

        def scratch(name, shape, dt):
            return nc.dram_tensor(name, shape, dt, kind="Internal").ap()

        kscr = scratch("kscr", [2, 3, D, CH], BF16)
        qscr = scratch("qscr", [3, D, S], BF16)
        mscr = scratch("mscr", [3, H, S], BF16)
        oscr = scratch("oscr", [H, S, DH], FP32)

        wk = [sb("wk_hi", [P, CI, D], FP32R), sb("wk_lo", [P, CI, D], FP32R)]
        wv = [sb("wv_hi", [P, CI, D], FP32R), sb("wv_lo", [P, CI, D], FP32R)]
        wq_sb, wh_sb, wout_sb = sb("wq_sb", [P, CI, D]), sb("wh_sb", [P, CI, D]), sb("wout_sb", [P, CI, D])
        wqkv_sb = sb("wqkv_sb", [P, CI, 3 * D])
        wg_sb, wu_sb = sb("wg_sb", [P, CI, HID]), sb("wu_sb", [P, CI, HID])
        wd_sb = sb("wd_sb", [P, HB, D])
        om_sb = sb("om_sb", [P, H // 2, P])
        bq_sb, bk_sb = sb("bq_sb", [P, CI]), sb("bk_sb", [P, CI])
        bv_sb, bh_sb, bout_sb = sb("bv_sb", [P, D]), sb("bh_sb", [P, D]), sb("bout_sb", [P, D])
        bqkv_sb = sb("bqkv_sb", [P, 3 * D])
        node, weight = sb("node", [P, 1]), sb("weight", [P, 1])
        node_neg, node_amp = sb("node_neg", [P, 1]), sb("node_amp", [P, 1])
        half_mask = sb("half_mask", [P, 2])
        head_mask = sb("head_mask", [P, H // 2])
        half_power, root_power = sb("half_power", [P, ST, 2 * H]), sb("root_power", [P, 1])
        ident = sb("ident", [P, P])
        causal = sb("causal", [P, 3 * P])

        ctx_raw = sb("ctx_raw", [P, CI, CH])
        ctx_hi = [sb(f"ctx_hi{i}", [P, CI, CH], FP32R) for i in range(2)]
        ctx_lo = [sb(f"ctx_lo{i}", [P, CI, CH], FP32R) for i in range(2)]
        kparts = sb("kparts", [P, 3, CI, CH], BF16)
        krest = sb("krest", [P, CH])
        kstack = [sb(f"kstack{i}", [P, H, CH], BF16) for i in range(2)]
        qparts = sb("qparts", [P, 3, CI, S], BF16)
        qnext, qstack = sb("qnext", [P, H, S], BF16), sb("qstack", [P, H, S], BF16)
        values = [sb(f"values{i}", [P, TT, H, 32]) for i in range(2)]
        probs = [sb(f"probs{i}", [P, GH * S]) for i in range(NPROB)]
        ksample = sb("ksample", [P, CI, H // 2, SAMPLE], BF16)
        chunk_max = sb("chunk_max", [P, ST, H, NCH])
        neg_max = sb("neg_max", [P, ST, H])
        mrest, mparts = sb("mrest", [H, S]), sb("mparts", [H, 3, S], BF16)
        den_in = sb("den_in", [P, 2, H])
        den_ok = sb("den_ok", [P, 2])
        verdict, verdict_int = sb("verdict", [1, 1]), sb("verdict_int", [1, 1], INT32)

        xs, xn = sb("xs", [P, ST, D]), sb("xn", [P, ST, D])
        xT = sb("xT", [P, CI, S])
        stats, mv = sb("stats", [P, ST, 6]), sb("mv", [P, ST, 2])
        veps, rstd = sb("veps", [P, ST]), sb("rstd", [P, ST])
        rden = sb("rden", [P, H])
        y = sb("y", [P, ST, D])
        qk = sb("qk", [P, ST, 2 * D])
        o_sb = qk[:, :, :].rearrange("p t (g s) -> p (t g) s", s=S)
        v1 = sb("v1", [P, ST, H, 32])
        ss, rnorm = sb("ss", [P, ST, 2 * H]), sb("rnorm", [P, ST, 2 * H])
        qkT = sb("qkT", [P, 4, S])
        feat = sb("feat", [P, 2, 2, S])
        kfeat = sb("kfeat", [P, 2, 2, S])
        amat = sb("amat", [P, GH, 3 * P])
        flat_amat = amat[:, :, :].rearrange("p a b -> p (a b)")
        hid = flat_amat.rearrange("p (k s) -> p k s", s=S)
        gate_e = kfeat[:, 0, :, :]
        wstage = feat[:, :, :, :].rearrange("p a b c -> p (a b c)")

        ps_s = [ctx.enter_context(nc.psum_tensor(f"ps_s{i}", [P, 1024], FP32)) for i in range(2)]
        ps_o = ctx.enter_context(nc.psum_tensor("ps_o", [P, 1024], FP32))
        ps_p = ctx.enter_context(nc.psum_tensor("ps_p", [P, 512], FP32))
        ps_a = ctx.enter_context(nc.psum_tensor("ps_a", [P, 512], FP32))

        w_in, b_in, late_in, om_in, i_in, w_ready = (
            sem(n) for n in ("w_in", "b_in", "late_in", "om_in", "i_in", "w_ready"))
        setup_dve, setup_pool, setup_pow = sem("setup_dve"), sem("setup_pool"), sem("setup_pow")
        judged = sem("judged")
        fast = Signals(sem, "f_", HEAD)
        general = Signals(sem, "g_", HEAD_GENERAL)

        block = ctx.enter_context(nc.Block())
        BS = NCH * STEPS

        def looped_passes(eng, body, p0=0):
            body(p0, 0, p0 // 2, True, False)
            with eng.Fori(0, NCH // 2 - 1) as c:
                body(c * 2 + (p0 + 1), 1, c + p0 // 2, False, False)
                body(c * 2 + (p0 + 2), 0, c + (p0 // 2 + 1), False, False)
            body(p0 + NCH - 1, 1, p0 // 2 + NCH // 2 - 1, False, True)

        def unrolled_passes(body):
            for p in range(NCH):
                body(p, p % 2, p // 2, p == 0, p == NCH - 1)

        def stages_at(step, table, behind=None):
            return [n for n in table if table[n] + (behind or {}).get(n, 0) == step]

        def head_of(b):
            return (b, b - 1, False)

        def tail_of(b):
            return (b + 2, b, True)

        def head_general(b):
            return (b, b, False)

        def tail_general(b):
            return (b + 1, b, True)

        @block.sync
        def _(sp):
            def reg(value):
                return value if isinstance(value, int) else sp.to_reg(value)

            def address(value):
                return value if isinstance(value, int) else sp.snap(value)

            def wait_all(*pairs):
                pairs = [(s, reg(v)) for s, v in pairs]
                for s, v in pairs:
                    sp.wait_ge(s, v)

            def load_ctx(c, ppb, q):
                b, t0 = address((q // ppb) % B), address((q % NCH) * CH)
                if not (isinstance(q, int) and q == 0):
                    wait_all((c["ctx_split"], q))
                src = ctxT.rearrange("b (i p) t -> p b i t", p=P)
                sp.dma_start(ctx_raw[:, :, :],
                             src[:, bass.ds(b, 1), :, bass.ds(t0, CH)].rearrange("p b i t -> p (b i) t")
                             ).then_inc(c["ctx_in"], 16)

            def stack_keys(c, q, par, used=None):
                written = reg(q * 48 + 48)
                used = used and (used[0], reg(used[1]))
                wait_all((c["k_parts"], q * 2 + 3))
                for i in range(3):
                    sp.dma_start(kscr[par, i].rearrange("(j p) t -> p j t", p=P),
                                 kparts[:, i, :, :]).then_inc(c["k_written"], 16)
                sp.wait_ge(c["k_written"], written)
                if used:
                    sp.wait_ge(*used)
                for n in range(SLOTS):
                    sp.dma_start(kstack[par][n * DH:(n + 1) * DH, :, :],
                                 kscr[par, KEY_PART[n]].rearrange("(h d) t -> d h t", d=DH)
                                 ).then_inc(c["k_stacked"][par], 16)

            def load_x(c, b, *waits):
                b = address(b)
                wait_all(*waits)
                sp.dma_start(xs[:, :, :],
                             x[bass.ds(b, 1), :, :].rearrange("b (i p) d -> p (b i) d", p=P)).then_inc(c["x_in"], 16)

            def stack_queries(c, clock, heads):
                written = reg(heads * 48 + 48)
                wait_all((c["operand"], c.at("operand", clock, "q")))
                for i in range(3):
                    sp.dma_start(qscr[i].rearrange("(j p) s -> p j s", p=P), qparts[:, i, :, :]
                                 ).then_inc(c["q_written"], 16)
                sp.wait_ge(c["q_written"], written)
                for n in range(SLOTS):
                    sp.dma_start(qnext[n * DH:(n + 1) * DH, :, :],
                                 qscr[QUERY_PART[n]].rearrange("(h d) s -> d h s", d=DH)).then_inc(c["q_stacked"], 16)

            def stack_shift(c, clock, heads):
                written = reg(heads * 48 + 48)
                wait_all((c["operand"], c.at("operand", clock, "maxT")))
                for i in range(3):
                    sp.dma_start(mscr[i], mparts[:, i, :]).then_inc(c["m_written"], 16)
                sp.wait_ge(c["m_written"], written)
                for i in range(3):
                    sp.dma_start(qnext[STACK + i:STACK + i + 1, :, :], mscr[i:i + 1]).then_inc(c["m_stacked"], 16)

            def regroup(c, clock, tails):
                written = reg(tails * 32 + 32)
                wait_all((c["operand"], c.at("operand", clock, "oT1")))
                for t in range(ST):
                    sp.dma_start(oscr[:, t * P:(t + 1) * P, :].rearrange("h s d -> s h d"),
                                 y[:, t, :].rearrange("p (h d) -> p h d", h=H)).then_inc(c["o_written"], 16)
                sp.wait_ge(c["o_written"], written)
                sp.dma_start(y[:, :, :], oscr.rearrange("(t a) (u s) d -> (a u) t (s d)", t=ST, u=S // DH)
                             ).then_inc(c["o_in"], 16)

            def store(c, clock, b):
                b = address(b)
                wait_all((c["operand"], c.at("operand", clock, "down")))
                sp.dma_start(out[bass.ds(b, 1), :, :].rearrange("b (i p) d -> p (b i) d", p=P),
                             y[:, :, :]).then_inc(c["stored"], 16)

            wr = lambda a: a.rearrange("(i p) n -> p i n", p=P)
            sp.sem_inc(fast["stored"], 16)
            sp.dma_start(wstage[:, 0:CI * D].rearrange("p (i n) -> p i n", i=CI), wr(wkT)).then_inc(w_in, 16)
            sp.dma_start(wstage[:, CI * D:2 * CI * D].rearrange("p (i n) -> p i n", i=CI), wr(wvT)).then_inc(w_in, 16)
            load_ctx(fast, NCH, 0)
            load_x(fast, 0)
            sp.dma_start(bk_sb[:, :], bk).then_inc(b_in, 16)
            sp.dma_start(bq_sb[:, :], bq).then_inc(b_in, 16)
            sp.dma_start(wq_sb[:, :, :], wr(wqT)).then_inc(b_in, 16)
            sp.dma_start(bv_sb[:, :], bv.partition_broadcast(P)).then_inc(b_in, 16)
            load_ctx(fast, NCH, 1)
            for dst, src in ((wh_sb, whT), (wout_sb, wout), (wqkv_sb, wqkv)):
                sp.dma_start(dst[:, :, :], wr(src)).then_inc(late_in, 16)
            for dst, src in ((bh_sb, bh), (bout_sb, bout), (bqkv_sb, bqkv)):
                sp.dma_start(dst[:, :], src.partition_broadcast(P)).then_inc(late_in, 16)
            for k in range(2 * R):
                r = k % R
                sp.dma_start(node[k * M:(k + 1) * M, :], nodes[r:r + 1].partition_broadcast(M)).then_inc(late_in, 16)
                sp.dma_start(weight[k * M:(k + 1) * M, :], weights[r:r + 1].partition_broadcast(M)).then_inc(late_in, 16)
            sp.wait_ge(setup_pool, 1)
            for h in range(H):
                row, col = (h % 8) * DH, (h % 2) * F
                sp.dma_start(om_sb[row:row + DH, h // 2, col:col + F],
                             omega[h * DH:(h + 1) * DH, :]).then_inc(om_in, 16)
            for dst, src in ((wg_sb, wgT), (wu_sb, wuT), (wd_sb, wdT)):
                sp.dma_start(dst[:, :, :].bitcast(INT32), wr(src)).then_inc(i_in, 16)
            sp.wait_ge(setup_dve, 1)
            stack_keys(fast, 0, 0)
            stack_queries(fast, (0, 0, False), 0)
            stack_shift(fast, (0, 0, False), 0)

            def fast_pass(b, tail):
                def body(p, par, half, first, last):
                    q = b * NCH + p
                    steps = b * BS + p * STEPS
                    load_ctx(fast, NCH, q + 2)
                    if not tail and last:
                        load_x(fast, 1, (fast["operand"], fast.at("operand", (0, 0, False), "ln0")))
                    if first and tail:
                        load_x(fast, b - 1, (fast["operand"], fast.at("operand", head_of(b), "ln0")))
                    stack_keys(fast, q + 1, 1 - par, (fast["exp_done"], steps + 2))
                    if tail and first:
                        regroup(fast, tail_of(b - 1), b - 1)
                    if tail and p == AT["down"] // STEPS:
                        store(fast, tail_of(b - 1), b - 1)
                        load_x(fast, (b + 1) % B, (fast["operand"], fast.at("operand", tail_of(b - 1), "down")))
                    if last:
                        stack_queries(fast, (b + 1, b, False), b + 1)
                        stack_shift(fast, (b + 1, b, False), b + 1)
                return body

            looped_passes(sp, fast_pass(0, False))
            with sp.Fori(1, B) as b:
                unrolled_passes(fast_pass(b, True))
            load_x(fast, B - 1, (fast["operand"], fast.at("operand", (B, B - 1, False), "ln0")))
            regroup(fast, tail_of(B - 1), B - 1)
            store(fast, tail_of(B - 1), B - 1)
            sp.wait_ge(fast["stored"], B * 16 + 16)
            sp.wait_ge(fast["k_stacked"][0], (B * NCH // 2 + 1) * 96)
            sp.wait_ge(fast["k_stacked"][1], (B * NCH // 2) * 96)
            sp.wait_ge(fast["ctx_in"], (B * NCH + 2) * 16)
            sp.wait_ge(fast["m_stacked"], (B + 1) * 48)
            sp.wait_ge(fast["q_stacked"], (B + 1) * 16 * SLOTS)
            sp.sem_inc(fast["landed"], 1)

            sp.wait_ge(judged, 3)
            with sp.If(sp.value_load(verdict_int[0:1, 0:1]) < 1):
                c = general
                sp.sem_inc(c["stored"], 16)
                load_ctx(c, 2 * NCH, 0)
                load_ctx(c, 2 * NCH, 1)
                stack_keys(c, 0, 0)
                with sp.Fori(0, B) as b:
                    load_x(c, b, (c["stored"], b * 16 + 16))
                    stack_queries(c, head_general(b), b)

                    def general_pass(attend):
                        def body(p, par, half, first, last):
                            q = b * (2 * NCH) + p
                            if attend and first:
                                used = (c["mscores"], b * BS + BS)
                            elif attend:
                                used = (c["scores"], b * BS + (p - NCH) * STEPS)
                            elif first:
                                used = (c["exp_done"], b * BS + 2)
                            else:
                                used = (c["mscores"], b * BS + p * STEPS)
                            load_ctx(c, 2 * NCH, q + 2)
                            stack_keys(c, q + 1, 1 - par, used)
                        return body

                    looped_passes(sp, general_pass(False))
                    stack_shift(c, head_general(b), b)
                    looped_passes(sp, general_pass(True), NCH)
                    load_x(c, b, (c["operand"], c.at("operand", head_general(b), "ln0")))
                    regroup(c, tail_general(b), b)
                    store(c, tail_general(b), b)
                sp.wait_ge(c["stored"], B * 16 + 16)
                sp.wait_ge(c["k_stacked"][0], (B * NCH + 1) * 96)
                sp.wait_ge(c["k_stacked"][1], (B * NCH) * 96)
                sp.wait_ge(c["ctx_in"], (2 * B * NCH + 2) * 16)

        @block.tensor
        def _(pe):
            mm = nc.tensor.matmul

            def project(c, unit, q, par):
                kind, j, part = unit
                hi, lo = ctx_hi[par], ctx_lo[par]
                if kind == "k":
                    k = part
                    for n, (w, a) in enumerate(((wk[0], hi), (wk[1], hi), (wk[0], lo))):
                        last = mm(ps_p[:, :], w[:, k, j * P:(j + 1) * P], a[:, k, :],
                                  start=(k == 0 and n == 0), stop=(k == CI - 1 and n == 2))
                    if part == CI - 1:
                        last.then_inc(c["k_proj"], 1)
                else:
                    for k in range(CI):
                        for n, (a, w) in enumerate(((hi, wv[0]), (lo, wv[0]), (hi, wv[1]))):
                            last = mm(ps_p[:, 0:D], a[:, k, j * P:(j + 1) * P], w[:, k, :],
                                      start=(k == 0 and n == 0), stop=(k == CI - 1 and n == 2))
                    last.then_inc(c["v_proj"], 1)

            def project_free(c, unit, q, vt):
                kind, j, part = unit
                if kind == "k" and part == 0:
                    pe.wait_ge(c["k_parts"], q * 2 + (j + 1))
                    if j == 0:
                        pe.wait_ge(c["ctx_split"], q + 1)
                        pe.wait_ge(c["v_ready"], vt + 1)
                elif kind == "v":
                    pe.wait_ge(c["v_ready"], vt + (j + 1))
                    if j == 0:
                        pe.wait_ge(c["k_parts"], q * 2 + 3)

            def transpose_blocks(src):
                for i in range(CI):
                    for s in range(ST):
                        last = nc.tensor.transpose(ps_a[:, i * S + s * P:i * S + (s + 1) * P],
                                                   src[:, s, i * P:(i + 1) * P], ident[:, :])
                return last

            def rows(w, n, col=0):
                for t in range(ST):
                    for k in range(CI):
                        last = mm(ps_a[:, t * n:(t + 1) * n], xT[:, k, t * P:(t + 1) * P], w[:, k, col:col + n],
                                  start=k == 0, stop=k == CI - 1)
                return last

            def stage(c, name, clock):
                pe.wait_ge(c["operand"], c.at("operand", clock, name) - 1)
                kind, n = name.rstrip("0123456789"), name[len(name.rstrip("0123456789")):]
                n = int(n) if n else 0
                if name in ("ln0T", "ln1T", "ln2T"):
                    last = transpose_blocks(xn)
                elif name == "q":
                    for j in range(CI):
                        for k in range(CI):
                            last = mm(ps_a[:, j * S:(j + 1) * S], wq_sb[:, k, j * P:(j + 1) * P], xT[:, k, :],
                                      start=k == 0, stop=k == CI - 1)
                elif kind == "max":
                    j, t = n // ST, n % ST
                    last = mm(ps_a[:, :], qparts[:, 0, j, t * P:(t + 1) * P],
                              ksample[:, j, :, :].rearrange("p h k -> p (h k)"), start=True, stop=True)
                elif name == "maxT":
                    for t in range(ST):
                        last = nc.tensor.transpose(ps_a[0:H, t * P:(t + 1) * P], neg_max[:, t, :], ident[:, :])
                elif kind in ("oT", "o2T"):
                    for g in range(G):
                        last = nc.tensor.transpose(ps_a[:, g * P:(g + 1) * P], o_sb[:, g, n * P:(n + 1) * P],
                                                   ident[:, :])
                elif name == "yT":
                    pe.wait_ge(c["o_in"], clock[1] * 16 + 16)
                    last = transpose_blocks(y)
                elif name == "y2T":
                    last = transpose_blocks(y)
                elif name == "wh":
                    last = rows(wh_sb, D)
                elif name == "wout":
                    last = rows(wout_sb, D)
                elif kind == "qk":
                    for k in range(CI):
                        last = mm(ps_a[:, :], xT[:, k, n * P:(n + 1) * P], wqkv_sb[:, k, 0:2 * D],
                                  start=k == 0, stop=k == CI - 1)
                elif name == "v":
                    last = rows(wqkv_sb, D, 2 * D)
                elif kind == "qkT":
                    for i in range(4):
                        last = nc.tensor.transpose(ps_a[:, i * P:(i + 1) * P], qk[:, n, i * P:(i + 1) * P],
                                                   ident[:, :])
                elif kind == "feat":
                    for i in range(2):
                        last = mm(ps_a[:, i * S:(i + 1) * S], om_sb[:, n, :], qkT[:, 2 * i + n // 4, :],
                                  start=True, stop=True)
                elif kind == "A":
                    p = n // 2
                    pe.wait_ge(c["kfeat"], c.at("kfeat", clock, f"feat{p}"))
                    mm(ps_a[:, 0:S], kfeat[:, p % 2, n % 2, 0:P], feat[:, p % 2, 0, :], start=True, stop=True)
                    last = mm(ps_a[:, S:S + P], kfeat[:, p % 2, n % 2, P:S], feat[:, p % 2, 0, P:S],
                              start=True, stop=True)
                elif kind == "pv":
                    for j in range(GH):
                        mm(ps_a[32 * j:32 * j + 32, 0:S], v1[:, 0, n * GH + j, :], amat[:, j, 0:S],
                           start=True, stop=False, skip_group_check=True)
                        last = mm(ps_a[32 * j:32 * j + 32, P:S], v1[:, 1, n * GH + j, :], amat[:, j, S:S + P],
                                  start=False, stop=True, skip_group_check=True)
                elif kind == "gu":
                    for i, w in enumerate((wg_sb, wu_sb)):
                        for k in range(CI):
                            last = mm(ps_a[:, i * S:(i + 1) * S], w[:, k, n * P:(n + 1) * P], xT[:, k, :],
                                      start=k == 0, stop=k == CI - 1)
                elif name == "down":
                    for t in range(ST):
                        for k in range(HB):
                            last = mm(ps_a[:, t * D:(t + 1) * D], hid[:, k, t * P:(t + 1) * P], wd_sb[:, k, :],
                                      start=k == 0, stop=k == HB - 1)
                last.then_inc(c["product"], 1)

            def products(c, names, clock):
                for name in names:
                    if name not in VECTOR_ONLY:
                        stage(c, name, clock)

            def value_product(c, n, s, par, starts, stops, vtile):
                i, g = s // G, s % G
                pe.wait_ge(c["exp_done"], n + 3)
                if g == 0:
                    pe.wait_ge(c["v_ready"], vtile + 2)
                for j in range(GH):
                    last = mm(ps_o[32 * j:32 * j + 32, g * S:(g + 1) * S],
                              values[par][:, i, g * GH + j, :], probs[s % NPROB][:, j * S:(j + 1) * S],
                              start=bool(starts and i == 0 and g % 2 == 0),
                              stop=bool(stops and i == TT - 1), skip_group_check=True)
                last.then_inc(c["pv_done"], 1)

            def attend_pass(c, q, n0, vt, stacked, par, first, last_chunk, next_values, at_step, out_free=None):
                pe.wait_ge(c["k_stacked"][par], stacked * 96 + 96)
                for s in range(STEPS):
                    i, g = s // G, s % G
                    pe.wait_ge(c["exp_done"], n0 + (s + 1))
                    for j in range(GH):
                        last = mm(ps_s[s % 2][:, j * S:(j + 1) * S],
                                  kstack[par][:, g * GH + j, i * P:(i + 1) * P],
                                  qstack[:, g * GH + j, :], start=True, stop=True)
                    last.then_inc(c["scores"], 1)
                    if s >= LAG:
                        if s == LAG and first and out_free is not None:
                            pe.wait_ge(c["operand"], out_free)
                        value_product(c, n0 + (s - LAG), s - LAG, par, first, last_chunk, vt + (s - LAG) // G)
                    elif not first:
                        value_product(c, n0 + (s - LAG), STEPS + s - LAG, 1 - par, False, False, vt + (-1))
                    if s in UNITS and (UNITS[s][0] == "k" or next_values):
                        project_free(c, UNITS[s], q + 1, vt + TT)
                        project(c, UNITS[s], q + 1, 1 - par)
                    at_step(s)
                if last_chunk:
                    for s in range(STEPS - LAG, STEPS):
                        value_product(c, n0 + s, s, par, False, True, vt + s // G)

            pe.sem_inc(fast["pv_done"], NPROB)
            pe.wait_ge(setup_dve, 2)
            pe.wait_ge(setup_pool, 4)
            for unit in UNITS.values():
                project_free(fast, unit, 0, 0)
                project(fast, unit, 0, 0)
            pe.wait_ge(b_in, 16 * 4)
            products(fast, HEAD, (0, 0, False))

            def fast_pass(b, tail):
                def body(p, par, half, first, last_chunk):
                    def at_step(s):
                        if not isinstance(p, int):
                            return
                        step = p * STEPS + s
                        if tail:
                            products(fast, stages_at(step, AT), tail_of(b - 1))
                        products(fast, stages_at(step, HEAD_AT if tail else HEAD_AT_FIRST), (b + 1, b, False))

                    if first:
                        pe.wait_ge(fast["operand"], fast.at("operand", head_of(b) if tail else (0, 0, False), "qcopy"))
                    attend_pass(fast, b * NCH + p, b * BS + p * STEPS, b * (NCH * TT) + p * TT,
                                b * (NCH // 2) + half, par, first, last_chunk, True, at_step,
                                fast.at("operand", tail_of(b - 1), "o") if tail else None)
                return body

            looped_passes(pe, fast_pass(0, False))
            pe.wait_ge(late_in, 16 * 14)
            pe.wait_ge(w_ready, 3)
            pe.wait_ge(om_in, 16 * H)
            with pe.Fori(1, B) as b:
                unrolled_passes(fast_pass(b, True))
            products(fast, TAIL, tail_of(B - 1))
            pe.wait_ge(judged, 1)
            nc.tensor.transpose(ps_a[0:1, 0:P], den_ok[:, 0:1], ident[:, :]).then_inc(judged, 1)

            pe.wait_ge(judged, 3)
            with pe.If(pe.value_load(verdict_int[0:1, 0:1]) < 1):
                c = general
                pe.sem_inc(c["pv_done"], NPROB)
                for unit in UNITS.values():
                    if unit[0] == "k":
                        project_free(c, unit, 0, 0)
                        project(c, unit, 0, 0)
                with pe.Fori(0, B) as b:
                    products(c, ["ln0T", "q"], head_general(b))

                    def maximum_pass(p, par, half, first, last_chunk):
                        pe.wait_ge(c["k_stacked"][par], (b * NCH + half) * 96 + 96)
                        if first:
                            pe.wait_ge(c["operand"], c.at("operand", head_general(b), "qcopy0"))
                        q, n0 = b * (2 * NCH) + p, b * BS + p * STEPS
                        for s in range(STEPS):
                            t, hp = s // (H // 2), s % (H // 2)
                            pe.wait_ge(c["mreduced"], n0 + (s + 1))
                            for j in range(2):
                                h = 2 * hp + j
                                last = mm(ps_s[s % 2][:, j * CH:(j + 1) * CH],
                                          qstack[0:STACK, h, t * P:(t + 1) * P], kstack[par][0:STACK, h, :],
                                          start=True, stop=True)
                            last.then_inc(c["mscores"], 1)
                            if s in UNITS and (UNITS[s][0] == "k" or last_chunk):
                                project_free(c, UNITS[s], q + 1, b * (NCH * TT))
                                project(c, UNITS[s], q + 1, 1 - par)

                    looped_passes(pe, maximum_pass)
                    products(c, ["maxT"], head_general(b))
                    pe.wait_ge(c["operand"], c.at("operand", head_general(b), "qcopy"))

                    def general_attend(p, par, half, first, last_chunk):
                        attend_pass(c, b * (2 * NCH) + p, b * BS + (p - NCH) * STEPS,
                                    b * (NCH * TT) + (p - NCH) * TT, b * NCH + half, par, first, last_chunk,
                                    not last_chunk, lambda s: None)

                    looped_passes(pe, general_attend, NCH)
                    products(c, TAIL, tail_general(b))

        @block.gpsimd
        def _(pool):
            pool.memset(om_sb[:, :, :], 0.0).then_inc(setup_pool, 1)
            pool.memset(ident[:, :], 0.0)
            pool.memset(causal[:, :], 1.0)
            pool.memset(head_mask[:, :], 1.0)
            pool.memset(half_power[:, :, :], -0.5)
            pool.memset(root_power[:, :], 0.5).then_inc(setup_pool, 1)
            pool.drain()
            pool.affine_select(out=ident[:, :], in_=ident[:, :], compare_op=ALU.not_equal, fill=1.0,
                               base=0, pattern=[[-1, P]], channel_multiplier=1).then_inc(setup_pool, 1)
            pool.affine_select(out=head_mask[:, :], in_=head_mask[:, :], compare_op=ALU.is_ge, fill=0.0,
                               base=0, pattern=[[-DH, H // 2]], channel_multiplier=1)
            pool.drain()
            pool.affine_select(out=head_mask[:, :], in_=head_mask[:, :], compare_op=ALU.is_ge, fill=0.0,
                               base=DH - 1, pattern=[[DH, H // 2]], channel_multiplier=-1)
            for k in (0, 2):
                blk = causal[:, k * P:(k + 1) * P]
                last = pool.affine_select(out=blk, in_=blk, compare_op=ALU.is_ge, fill=0.0,
                                          base=0, pattern=[[1, P]], channel_multiplier=-1)
            last.then_inc(setup_pool, 1)

            def power(c, name, clock):
                pool.wait_ge(c["variance"], c.at("powered", clock, name))
                if name == "v":
                    pool.tensor_tensor(rnorm[:, :, :], ss[:, :, :], half_power[:, :, :], ALU.pow
                                       ).then_inc(c["powered"], 1)
                else:
                    pool.tensor_tensor(rstd[:, :], veps[:, :], half_power[:, :, 0], ALU.pow
                                       ).then_inc(c["powered"], 1)

            def tail(c, clock):
                power(c, "wh", clock)
                power(c, "v", clock)
                for p in range(H // 2):
                    pool.wait_ge(c["acted"], c.at("acted", clock, f"feat{p}"))
                    for k in range(2):
                        last = pool.tensor_tensor(kfeat[:, p % 2, k, :], feat[:, p % 2, 1, :],
                                                  half_mask[:, k:k + 1].to_broadcast([P, S]), ALU.mult)
                    last.then_inc(c["kfeat"], 1)
                power(c, "wout", clock)

            power(fast, "ln0", (0, 0, False))
            pool.wait_ge(setup_pow, 1)
            pool.tensor_tensor(node_amp[:, :], node_amp[:, :], root_power[:, :], ALU.pow).then_inc(setup_pow, 1)
            power(fast, "ln0", (1, 0, False))
            with pool.Fori(1, B) as b:
                tail(fast, tail_of(b - 1))
                power(fast, "ln0", (b + 1, b, False))
            tail(fast, tail_of(B - 1))
            pool.wait_ge(judged, 3)
            with pool.If(pool.value_load(verdict_int[0:1, 0:1]) < 1):
                with pool.Fori(0, B) as b:
                    power(general, "ln0", head_general(b))
                    tail(general, tail_general(b))

        @block.scalar
        def _(act):
            def probabilities(c, n, s):
                act.wait_ge(c["scores"], n + 1)
                act.wait_ge(c["pv_done"], n + 1)
                nc.scalar.activation(probs[s % NPROB][:, :], ps_s[s % 2][:, :], ACT.Exp,
                                     scale=float(DH) ** -0.5).then_inc(c["exp_done"], 1)

            def stage(c, name, clock):
                if name in FEATS:
                    p = FEATS.index(name)
                    act.wait_ge(c["args"], c.at("args", clock, name))
                    nc.scalar.activation(feat[:, p % 2, :, :], feat[:, p % 2, :, :], ACT.Exp).then_inc(c["acted"], 1)
                else:
                    k = GATES.index(name)
                    act.wait_ge(c["product"], c.at("product", clock, name))
                    nc.scalar.activation(gate_e[:, k % 2, :], ps_a[:, 0:S], ACT.Exp, scale=-1.0
                                         ).then_inc(c["acted"], 1)

            def loop_of_steps(c, b):
                with act.Fori(0, NCH) as p:
                    for s in range(STEPS):
                        probabilities(c, b * BS + p * STEPS + s, s)

            act.sem_inc(fast["exp_done"], 2)
            loop_of_steps(fast, 0)
            mine = {n: AT[n] for n in FEATS + GATES}
            with act.Fori(1, B) as b:
                for step in range(BS):
                    probabilities(fast, b * BS + step, step % STEPS)
                    for name in stages_at(step, mine, ACT_BEHIND):
                        stage(fast, name, tail_of(b - 1))
            for name in FEATS + GATES:
                stage(fast, name, tail_of(B - 1))
            act.wait_ge(judged, 3)
            with act.If(act.value_load(verdict_int[0:1, 0:1]) < 1):
                act.sem_inc(general["exp_done"], 2)
                with act.Fori(0, B) as b:
                    loop_of_steps(general, b)
                    for name in FEATS + GATES:
                        stage(general, name, tail_general(b))

        @block.vector
        def _(dve):
            v = nc.vector

            def cut(hi, lo, src):
                v.tensor_copy(hi, src)
                dve.drain()
                return v.tensor_tensor(lo, src, hi.bitcast(FP32), ALU.subtract)

            def split_ctx(c, q, par):
                dve.wait_ge(c["ctx_in"], q * 16 + 16)
                cut(ctx_hi[par][:, :, :], ctx_lo[par][:, :, :], ctx_raw[:, :, :]).then_inc(c["ctx_split"], 1)

            def keys_out(c, q, j):
                dve.wait_ge(c["k_proj"], q * 2 + (j + 1))
                if j == 0 and not (isinstance(q, int) and q == 0):
                    dve.wait_ge(c["k_written"], q * 48)
                bias = bk_sb[:, j:j + 1]
                v.tensor_scalar(kparts[:, 0, j, :], ps_p[:, :], bias, None, ALU.add)
                dve.drain()
                v.scalar_tensor_tensor(krest[:, :], ps_p[:, :], bias, kparts[:, 0, j, :], ALU.add, ALU.subtract)
                dve.drain()
                v.tensor_copy(kparts[:, 1, j, :], krest[:, :])
                dve.drain()
                v.tensor_tensor(kparts[:, 2, j, :], krest[:, :], kparts[:, 1, j, :], ALU.subtract
                                ).then_inc(c["k_parts"], 1)

            def values_out(c, vt, tile, par, steps_before):
                dve.wait_ge(c["v_proj"], vt + (tile + 1))
                if tile == 0 and steps_before is not None:
                    dve.wait_ge(c["pv_done"], steps_before + NPROB)
                v.tensor_tensor(values[par][:, tile, :, 0:DH],
                                ps_p[:, 0:D].rearrange("p (h d) -> p h d", h=H),
                                bv_sb[:, :].rearrange("p (h d) -> p h d", h=H), ALU.add).then_inc(c["v_ready"], 1)

            def layernorm(c, name, clock):
                for t in range(ST):
                    v.bn_stats(stats[:, t, :], xs[:, t, :])
                dve.drain()
                for t in range(ST):
                    v.bn_aggr(mv[:, t, :], stats[:, t, :])
                dve.drain()
                v.tensor_scalar(veps[:, :], mv[:, :, 1], EPS, None, ALU.add).then_inc(c["variance"], 1)
                dve.wait_ge(c["powered"], c.at("powered", clock, name))
                for t in range(ST):
                    last = v.tensor_scalar(xn[:, t, :], xs[:, t, :], mv[:, t, 0:1], rstd[:, t:t + 1],
                                           ALU.subtract, ALU.mult)
                return last

            def residual(c, bias):
                v.tensor_tensor(xs[:, :, :], xs[:, :, :], ps_a[:, :].rearrange("p (t d) -> p t d", t=ST), ALU.add)
                dve.drain()
                v.tensor_tensor(xs[:, :, :], xs[:, :, :],
                                bias[:, :].unsqueeze(1).to_broadcast([P, ST, D]), ALU.add)
                dve.drain()

            def normalise(t, floor):
                heads = ps_a[:, :].rearrange("p (h c) -> p h c", c=32)
                if floor is None:
                    v.tensor_scalar(den_in[:, 0, :], heads[:, :, DH], DEN_LEAST, DEN_MOST, ALU.max, ALU.min)
                    v.reciprocal(rden[:, :], heads[:, :, DH])
                    dve.drain()
                    v.tensor_tensor(den_in[:, 1, :], den_in[:, 0, :], heads[:, :, DH], ALU.is_equal)
                    dve.drain()
                    v.tensor_reduce(den_ok[:, 1:2], den_in[:, 1, :], AX.X, ALU.min)
                    dve.drain()
                    v.tensor_tensor(den_ok[:, 0:1], den_ok[:, 0:1], den_ok[:, 1:2], ALU.min)
                else:
                    v.tensor_scalar(rden[:, :], heads[:, :, DH], floor, None, ALU.max)
                    dve.drain()
                    v.reciprocal(rden[:, :], rden[:, :])
                    dve.drain()
                return v.tensor_tensor(y[:, t, :].rearrange("p (h d) -> p h d", d=DH), heads[:, :, 0:DH],
                                       rden[:, :].unsqueeze(2).to_broadcast([P, H, DH]), ALU.mult)

            def stage(c, name, clock):
                heads, tails, is_tail = clock
                kind, n = name.rstrip("0123456789"), name[len(name.rstrip("0123456789")):]
                n = int(n) if n else 0
                if name not in VECTOR_ONLY:
                    dve.wait_ge(c["product"], c.at("product", clock, name))
                if name == "ln0":
                    dve.wait_ge(c["x_in"], c.at("x_in", clock, "x") * 16)
                    last = layernorm(c, name, clock)
                elif name in ("ln0T", "ln1T", "ln2T", "yT", "y2T"):
                    last = v.tensor_copy(xT[:, :, :], ps_a[:, :].rearrange("p (i s) -> p i s", i=CI))
                elif name == "q":
                    dve.wait_ge(c["stored"], tails * 16 + 16)
                    for j in range(CI):
                        src, bias = ps_a[:, j * S:(j + 1) * S], bq_sb[:, j:j + 1]
                        v.tensor_scalar(qparts[:, 0, j, :], src, bias, None, ALU.add)
                        dve.drain()
                        v.scalar_tensor_tensor(y[:, j, :], src, bias, qparts[:, 0, j, :], ALU.add, ALU.subtract)
                    dve.drain()
                    v.tensor_copy(qparts[:, 1, :, :], y[:, :, :])
                    dve.drain()
                    last = v.tensor_tensor(qparts[:, 2, :, :], y[:, :, :], qparts[:, 1, :, :], ALU.subtract)
                elif name == "kbd":
                    for j in range(CI):
                        last = v.tensor_tensor(ksample[:, j, :, :],
                                               kparts[:, 0, j, 0:SAMPLE].unsqueeze(1).to_broadcast([P, H // 2, SAMPLE]),
                                               head_mask[:, :].unsqueeze(2).to_broadcast([P, H // 2, SAMPLE]), ALU.mult)
                elif kind == "max":
                    j, t = n // ST, n % ST
                    last = v.tensor_reduce(neg_max[:, t, j * (H // 2):(j + 1) * (H // 2)],
                                           ps_a[:, :].rearrange("p (h k) -> p h k", k=SAMPLE), AX.X, ALU.max,
                                           negate=True)
                elif name == "fullmax":
                    last = v.tensor_reduce(neg_max[:, :, :], chunk_max[:, :, :, :], AX.X, ALU.max, negate=True)
                elif name == "maxT":
                    src = ps_a[0:H, 0:S]
                    v.tensor_copy(mparts[:, 0, :], src)
                    dve.drain()
                    v.tensor_tensor(mrest[:, :], src, mparts[:, 0, :], ALU.subtract)
                    dve.drain()
                    v.tensor_copy(mparts[:, 1, :], mrest[:, :])
                    dve.drain()
                    last = v.tensor_tensor(mparts[:, 2, :], mrest[:, :], mparts[:, 1, :], ALU.subtract)
                elif name in ("qcopy", "qcopy0"):
                    dve.wait_ge(c["q_stacked"], heads * (16 * SLOTS) + 16 * SLOTS)
                    if name == "qcopy":
                        dve.wait_ge(c["m_stacked"], heads * 48 + 48)
                    last = v.tensor_copy(qstack[:, :, :], qnext[:, :, :])
                elif name == "o":
                    dve.wait_ge(c["pv_done"], tails * BS + (BS + NPROB))
                    last = v.tensor_copy(o_sb[:, :, :], ps_o[:, :].rearrange("p (g s) -> p g s", g=G))
                elif kind == "oT":
                    last = normalise(n, None)
                elif kind == "o2T":
                    last = normalise(n, 1e-6)
                elif name in ("wh", "wout"):
                    if name == "wh":
                        dve.wait_ge(c["x_in"], c.at("x_in", clock, "x") * 16)
                    residual(c, bh_sb if name == "wh" else bout_sb)
                    last = layernorm(c, name, clock)
                elif kind == "qk":
                    last = v.tensor_tensor(qk[:, n, :], ps_a[:, :], bqkv_sb[:, 0:2 * D], ALU.add)
                elif name == "v":
                    for t in range(ST):
                        v.tensor_tensor(v1[:, t, :, 0:DH], ps_a[:, t * D:(t + 1) * D].rearrange("p (h d) -> p h d", h=H),
                                        bqkv_sb[:, 2 * D:3 * D].rearrange("p (h d) -> p h d", h=H), ALU.add)
                    sq = feat[:, :, :, :].rearrange("p a b s -> p (a b s)").rearrange("p (t n) -> p t n", t=ST)
                    v.tensor_tensor(sq, qk[:, :, :], qk[:, :, :], ALU.mult)
                    dve.drain()
                    v.tensor_reduce(ss[:, :, :].rearrange("p t h -> p (t h)"),
                                    sq.rearrange("p t (h d) -> p (t h) d", d=DH), AX.X, ALU.add)
                    dve.drain()
                    v.tensor_scalar(ss[:, :, :], ss[:, :, :], 1e-24, None, ALU.max).then_inc(c["variance"], 1)
                    dve.wait_ge(c["powered"], c.at("powered", clock, name))
                    qk3 = qk[:, :, :].rearrange("p t (h d) -> p (t h) d", d=DH)
                    last = v.tensor_tensor(qk3, qk3, rnorm[:, :, :].rearrange("p t h -> p (t h)").unsqueeze(2)
                                           .to_broadcast([P, ST * 2 * H, DH]), ALU.mult)
                elif kind == "qkT":
                    last = v.tensor_copy(qkT[:, :, n * P:(n + 1) * P], ps_a[:, :].rearrange("p (i s) -> p i s", i=4))
                elif kind == "feat":
                    f = feat[:, n % 2, :, :].rearrange("p a s -> p (a s)")
                    v.tensor_scalar(f, ps_a[:, :], node_amp[:, :], node_neg[:, :], ALU.mult, ALU.add
                                    ).then_inc(c["operand"], 1)
                    dve.drain()
                    v.tensor_scalar(f, f, 20.0, -20.0, ALU.min, ALU.max).then_inc(c["args"], 1)
                    return
                elif kind == "A":
                    last = v.tensor_tensor(amat[:, n % GH, :], ps_a[:, 0:3 * P], causal[:, :], ALU.mult)
                elif kind == "pv":
                    last = v.tensor_copy(o_sb[:, n, :], ps_a[:, 0:S])
                elif kind == "gu":
                    dve.wait_ge(c["acted"], c.at("acted", clock, name))
                    e = gate_e[:, n % 2, :]
                    v.tensor_scalar(e, e, 1.0, None, ALU.add)
                    dve.drain()
                    v.reciprocal(e, e)
                    dve.drain()
                    v.tensor_tensor(e, e, ps_a[:, 0:S], ALU.mult)
                    dve.drain()
                    last = v.tensor_tensor(hid[:, n, :], e, ps_a[:, S:2 * S], ALU.mult)
                elif name == "down":
                    last = v.tensor_tensor(y[:, :, :], xs[:, :, :], ps_a[:, :].rearrange("p (t d) -> p t d", t=ST),
                                           ALU.add)
                last.then_inc(c["operand"], 1)

            for i in range(2):
                v.memset(kstack[i][STACK:P, :, :], 1.0)
                v.memset(values[i][:, :, :, DH:32], 0.0)
            v.memset(qnext[STACK:P, :, :], 0.0)
            v.memset(v1[:, :, :, DH:32], 0.0)
            v.memset(half_mask[:, :], 0.0)
            v.memset(den_ok[:, 0:1], 1.0)
            dve.drain()
            for i in range(2):
                v.memset(values[i][:, :, :, DH:DH + 1], 1.0)
            v.memset(v1[:, :, :, DH:DH + 1], 1.0).then_inc(setup_dve, 1)
            dve.sem_inc(fast["k_parts"], 1)
            dve.sem_inc(fast["v_ready"], 1)
            dve.wait_ge(w_in, 32)
            for n, w in enumerate((wk, wv)):
                src = wstage[:, n * CI * D:(n + 1) * CI * D].rearrange("p (i n) -> p i n", i=CI)
                cut(w[0][:, :, :], w[1][:, :, :], src)
            dve.drain()
            dve.sem_inc(setup_dve, 1)
            split_ctx(fast, 0, 0)
            dve.wait_ge(b_in, 16 * 4)
            dve.wait_ge(setup_pool, 4)
            for j in range(CI):
                keys_out(fast, 0, j)
            for tile in range(TT):
                values_out(fast, 0, tile, 0, None)
            for name in HEAD[:-1]:
                stage(fast, name, (0, 0, False))
            split_ctx(fast, 1, 1)
            stage(fast, HEAD[-1], (0, 0, False))

            def setup_tail():
                dve.wait_ge(late_in, 16 * 14)
                v.tensor_scalar(node_amp[:, :], node[:, :], 0.0, 2.0, ALU.max, ALU.mult).then_inc(setup_pow, 1)
                v.tensor_scalar(node_neg[:, :], node[:, :], -1.0, None, ALU.mult)
                for k in range(2):
                    v.tensor_scalar(half_mask[k * F:(k + 1) * F, k:k + 1], weight[k * F:(k + 1) * F, :],
                                    0.0, 1.0 / M, ALU.max, ALU.mult)
                dve.wait_ge(i_in, 16 * 3)
                for dst in (wg_sb, wu_sb, wd_sb):
                    v.tensor_scalar(dst[:, :, :], dst[:, :, :].bitcast(INT32), QUANT, None, ALU.mult
                                    ).then_inc(w_ready, 1)
                dve.wait_ge(setup_pow, 2)

            def fast_pass(b, tail):
                def body(p, par, half, first, last_chunk):
                    q = b * NCH + p
                    for s in range(STEPS):
                        if s in UNITS:
                            kind, j, part = UNITS[s]
                            if kind == "k" and part == CI - 1:
                                keys_out(fast, q + 1, j)
                            if kind == "v":
                                values_out(fast, b * (NCH * TT) + (p + 1) * TT, j, 1 - par, b * BS + p * STEPS)
                        if s == STEPS - 3:
                            split_ctx(fast, q + 2, par)
                        if isinstance(p, int):
                            if tail:
                                for name in stages_at(p * STEPS + s, AT):
                                    stage(fast, name, tail_of(b - 1))
                            for name in stages_at(p * STEPS + s, HEAD_AT if tail else HEAD_AT_FIRST):
                                stage(fast, name, (b + 1, b, False))
                    if last_chunk:
                        dve.wait_ge(fast["scores"], b * BS + BS)
                        stage(fast, "qcopy", (b + 1, b, False))
                return body

            setup_tail()
            looped_passes(dve, fast_pass(0, False))
            with dve.Fori(1, B) as b:
                unrolled_passes(fast_pass(b, True))
            for name in TAIL:
                stage(fast, name, tail_of(B - 1))
            dve.drain()
            dve.sem_inc(judged, 1)
            dve.wait_ge(judged, 2)
            v.tensor_reduce(verdict[:, :], ps_a[0:1, 0:P], AX.X, ALU.min)
            dve.drain()
            dve.wait_ge(fast["landed"], 1)
            v.tensor_copy(verdict_int[:, :], verdict[:, :]).then_inc(judged, 1)

            dve.wait_ge(judged, 3)
            with dve.If(dve.value_load(verdict_int[0:1, 0:1]) < 1):
                c = general
                dve.sem_inc(c["k_parts"], 1)
                dve.sem_inc(c["v_ready"], 1)
                dve.sem_inc(c["mreduced"], 2)
                split_ctx(c, 0, 0)
                for j in range(CI):
                    keys_out(c, 0, j)
                split_ctx(c, 1, 1)
                with dve.Fori(0, B) as b:
                    for name in ("ln0", "ln0T", "q", "qcopy0"):
                        stage(c, name, head_general(b))

                    def maximum_pass(p, par, half, first, last_chunk):
                        q, n0 = b * (2 * NCH) + p, b * BS + p * STEPS
                        for s in range(STEPS):
                            t, hp = s // (H // 2), s % (H // 2)
                            dve.wait_ge(c["mscores"], n0 + (s + 1))
                            v.tensor_reduce(chunk_max[:, t, 2 * hp:2 * hp + 2, bass.ds(p, 1)],
                                            ps_s[s % 2][:, :].rearrange("p (h t) -> p h t", h=2), AX.X, ALU.max
                                            ).then_inc(c["mreduced"], 1)
                            if s in UNITS:
                                kind, j, part = UNITS[s]
                                if kind == "k" and part == CI - 1:
                                    keys_out(c, q + 1, j)
                                if kind == "v" and last_chunk:
                                    values_out(c, b * (NCH * TT), j, 1 - par, b * BS)
                        split_ctx(c, q + 2, par)

                    looped_passes(dve, maximum_pass)
                    dve.drain()
                    for name in ("fullmax", "maxT", "qcopy"):
                        stage(c, name, head_general(b))

                    def general_attend(p, par, half, first, last_chunk):
                        q = b * (2 * NCH) + p
                        for j in range(CI):
                            keys_out(c, q + 1, j)
                        if not last_chunk:
                            for tile in range(TT):
                                values_out(c, b * (NCH * TT) + (p - NCH + 1) * TT, tile, 1 - par,
                                           b * BS + (p - NCH) * STEPS)
                        split_ctx(c, q + 2, par)

                    looped_passes(dve, general_attend, NCH)
                    for name in TAIL:
                        stage(c, name, tail_general(b))


def kernel(**inputs):
    import numpy as np
    import concourse.bacc as bacc
    from concourse.bass_utils import run_bass_kernel_spmd

    i = {k: np.asarray(a) for k, a in inputs.items()}
    omega = i["L0_attn_omega"]
    arrays = {
        "x": i["x"], "ctxT": i["ctx_1024"].transpose(0, 2, 1),
        "wqT": i["L0_xattn_Wq"].T, "bq": i["L0_xattn_bq"].reshape(CI, P).T, "wkT": i["L0_xattn_Wk"].T, "bk": i["L0_xattn_bk"].reshape(CI, P).T,
        "wvT": i["L0_xattn_Wv"].T, "bv": i["L0_xattn_bv"], "whT": i["L0_xattn_Wh"].T, "bh": i["L0_xattn_bh"],
        "wqkv": i["L0_attn_Wqkv"], "bqkv": i["L0_attn_bqkv"], "wout": i["L0_attn_Wout"], "bout": i["L0_attn_bout"],
        "omega": omega.transpose(1, 2, 0, 3).reshape(H * DH, F),
        "nodes": i["L0_attn_quad_nodes"], "weights": i["L0_attn_quad_weights"],
        "wgT": i["L0_ffn_w_gate"].T, "wuT": i["L0_ffn_w_up"].T, "wdT": i["L0_ffn_w_down"].T,
    }
    arrays = {k: np.ascontiguousarray(a) for k, a in arrays.items()}
    nc = bacc.Bacc("TRN2", target_bir_lowering=False, num_devices=1)
    aps = [nc.dram_tensor(k, a.shape, mybir.dt.from_np(a.dtype), kind="ExternalInput").ap()
           for k, a in arrays.items()]
    out = nc.dram_tensor("out", (B, S, D), FP32, kind="ExternalOutput").ap()
    perceiver(nc, *aps, out)
    r = run_bass_kernel_spmd(nc, [arrays], core_ids=[0])
    return r.results[0]["out"]
```

```python
import concourse.bass as bass
from concourse import mybir
from contextlib import ExitStack

FP32 = mybir.dt.float32
FP32R = mybir.dt.float32r
BF16 = mybir.dt.bfloat16
INT32 = mybir.dt.int32
ALU = mybir.AluOpType
ACT = mybir.ActivationFunctionType
AX = mybir.AxisListType

B, S, D = 4, 256, 256
T = 4096
H = 16
DH = D // H
P = 128
CI = D // P
ST = S // P
CH = 512
NCH = T // CH
TT = CH // P
GH = 4
G = H // GH
STEPS = TT * G
M, R = 32, 2
F = R * M
HID = 768
HB = HID // P
EPS = 1e-5
QUANT = 1.0 / 127.0
KEY_PART = (0, 0, 0, 1, 1, 2)
QUERY_PART = (0, 1, 2, 0, 1, 0)
SLOTS = len(KEY_PART)
STACK = SLOTS * DH

LAG = 2
NPROB = 4
BANKS_ALONE = 4
SAMPLE = 64
DEN_LEAST, DEN_MOST = 2.0 ** -40, 2.0 ** 40

UNITS = {0: ("k", 0, 0), 1: ("k", 0, 1), 4: ("k", 1, 0), 5: ("k", 1, 1),
         8: ("v", 0, 0), 10: ("v", 1, 0), 12: ("v", 2, 0), 13: ("v", 3, 0)}

PROLOGUE = ["ln0", ("k", 0, 0), ("k", 0, 1), "ln0T", ("k", 1, 0), ("k", 1, 1), "q", "kbd",
            "max0", ("v", 0, 0), "max1", ("v", 1, 0), "max2", ("v", 2, 0), "max3", ("v", 3, 0), "maxT"]

SPLIT, SPLIT_LAST = 7, 13

VECTOR_ONLY = ("ln0", "kbd", "qcopy", "qcopy0", "fullmax", "o", "ss0", "ss1", "norm0", "norm1",
               *(f"gate{k}" for k in range(HB)))
HEAD = ["ln0", "ln0T", "q", "kbd", "max0", "max1", "max2", "max3", "maxT", "qcopy"]
HEAD_GENERAL = ["ln0", "ln0T", "q", "qcopy0", "fullmax", "maxT", "qcopy"]
TAIL_STEPS = [("o", 0), ("oT0", 3), ("oT1", 1), ("yT", 10), ("wh", 1), ("ln1T", 4), ("qk0", 1), ("ss0", 0),
              ("qk1", 1), ("ss1", 0), ("v", 1), ("norm0", 3), ("norm1", 4), ("qkT0", 1), ("qkT1", 3),
              ("feat0", 1), ("feat1", 1)]
for _g in range(G):
    TAIL_STEPS += [(f"feat{2 * _g + 1}", 1)] if _g else []
    TAIL_STEPS += [(f"A{4 * _g}", 2 if _g < 2 else 1), (f"A{4 * _g + 1}", 1)]
    TAIL_STEPS += [(f"feat{2 * _g + 2}", 1)] if _g < G - 1 else []
    TAIL_STEPS += [(f"A{4 * _g + 2}", 1), (f"A{4 * _g + 3}", 1), (f"pv{_g}", 1)]
TAIL_STEPS += [("o2T0", 1), ("o2T1", 1), ("y2T", 1), ("wout", 1), ("ln2T", 4)]
for _k in range(HB):
    TAIL_STEPS += [(f"gu{_k}", 2), (f"gate{_k}", 1)]
TAIL_STEPS += [("down", 4)]
TAIL = [name for name, _ in TAIL_STEPS]
KEYS_STEPS = (2, 6, 7)


def spread(stages):
    at, step = {}, 0
    for name, behind in stages:
        step += behind
        while step % STEPS in KEYS_STEPS and behind:
            step += 1
        at[name] = step
    return at


AT = spread(TAIL_STEPS)
NORMALISED = TAIL.index("oT1") + 1
FEATS = [f"feat{p}" for p in range(H // 2)]
GATES = [f"gu{k}" for k in range(HB)]
HEAD_AT = {"ln0": 110, "ln0T": 113, "q": 115, "kbd": 119, "max0": 120, "max1": 121, "max2": 122, "max3": 123,
           "maxT": 124}
HEAD_AT_FIRST = {**HEAD_AT, "ln0": 112, "ln0T": 114, "q": 116}
ACT_BEHIND = {**{n: 2 for n in FEATS}, **{n: 1 for n in GATES}}
NEEDS = {"maxT": "max3", "oT0": "o", "oT1": "o", "qk1": "ln1T", "v": "ln1T", "qkT0": "norm0", "qkT1": "norm1",
         **{n: "qkT1" for n in FEATS}, **{f"A{h}": "qkT1" for h in range(H)},
         **{f"pv{g}": f"A{GH * g + GH - 1}" for g in range(G)}, "o2T0": "pv3", "o2T1": "pv3",
         **{f"gu{k}": f"gate{k - 2}" if k >= 2 else "ln2T" for k in range(HB)},
         **{f"max{n}": "kbd" for n in range(4)}}


class Signals(dict):

    NAMES = ("ctx_in", "ctx_split",
             "k_proj", "v_proj",
             "k_out", "k_parts", "v_ready",
             "k_written",
             "scores", "exp_done", "pv_done",
             "mscores", "mreduced",
             "x_in", "q_written", "q_stacked", "q_ready", "o_written", "o_in", "stored",
             "product", "operand",
             "variance", "powered",
             "acted", "kfeat",
             "landed")

    def __init__(self, sem, prefix, head):
        for name in self.NAMES:
            self[name] = sem(prefix + name)
        self["k_stacked"] = [sem(prefix + "k_stacked0"), sem(prefix + "k_stacked1")]
        self.stages = {
            "product": ([n for n in head if n not in VECTOR_ONLY], [n for n in TAIL if n not in VECTOR_ONLY]),
            "operand": (head, TAIL),
            "powered": (["ln0"], ["wh", "norm0", "norm1", "wout"]),
            "acted": ([], FEATS + GATES), "kfeat": ([], [f"A{h}" for h in range(H)]),
            "x_in": (["x"], ["x"]),
        }

    def at(self, kind, clock, name):
        heads, tails, is_tail = clock
        per_head, per_tail = self.stages[kind]
        total = (per_tail if is_tail else per_head).index(name) + 1
        if per_head:
            total = heads * len(per_head) + total
        if per_tail:
            total = tails * len(per_tail) + total
        return total


    def ready(self, clock, name, banks):
        stages, products = self.stages["operand"][clock[2]], self.stages["product"][clock[2]]
        i, k = stages.index(name), products.index(name)
        need = NEEDS.get(name)
        i = stages.index(need) if need in stages else i - 1
        if k >= banks:
            i = max(i, stages.index(products[k - banks]))
        return self.at("operand", clock, stages[i])


def perceiver(nc, x, ctxT, wqT, bq, wkT, bk, wvT, bv, whT, bh, wqkv, bqkv, wout, bout,
              omega, nodes, weights, wgT, wuT, wdT, out):
    ctx = ExitStack()
    with ctx:
        def sb(name, shape, dt=FP32):
            return ctx.enter_context(nc.sbuf_tensor(name, shape, dt))

        def sem(name):
            return ctx.enter_context(nc.semaphore(name))

        def scratch(name, shape, dt):
            return nc.dram_tensor(name, shape, dt, kind="Internal").ap()

        kscr = scratch("kscr", [3, D, CH], BF16)
        qscr = scratch("qscr", [3, D, S], BF16)
        oscr = scratch("oscr", [H, S, DH], FP32)

        wk = [sb("wk_hi", [P, CI, D], FP32R), sb("wk_lo", [P, CI, D], FP32R)]
        wv = [sb("wv_hi", [P, CI, D], FP32R), sb("wv_lo", [P, CI, D], FP32R)]
        wq_sb, wh_sb, wout_sb = sb("wq_sb", [P, CI, D]), sb("wh_sb", [P, CI, D]), sb("wout_sb", [P, CI, D])
        wqkv_sb = sb("wqkv_sb", [P, CI, 3 * D])
        wg_r, wu_r, wd_sb = sb("wg", [P, CI, HID], FP32R), sb("wu", [P, CI, HID], FP32R), sb("wd_sb", [P, HB, D])
        om_sb = sb("om_sb", [P, H // 2, P])
        bq_sb, bk_sb = sb("bq_sb", [P, CI]), sb("bk_sb", [P, CI])
        bv_sb, bh_sb, bout_sb = sb("bv_sb", [P, D]), sb("bh_sb", [P, D]), sb("bout_sb", [P, D])
        bqkv_sb = sb("bqkv_sb", [P, 3 * D])
        node, weight = sb("node", [P, 1]), sb("weight", [P, 1])
        node_neg, clip_most, clip_least = sb("node_neg", [P, 1]), sb("clip_most", [P, 1]), sb("clip_least", [P, 1])
        node_amp = sb("node_amp", [P, R])
        half_mask = sb("half_mask", [P, 2])
        head_mask = sb("head_mask", [P, H // 2])
        half_power, root_power = sb("half_power", [P, ST, 2 * H]), sb("root_power", [P, R])
        ident = sb("ident", [P, P])
        causal = sb("causal", [P, 3 * P])

        ctx_raw = sb("ctx_raw", [P, CI, CH])
        ctx_hi = [sb(f"ctx_hi{i}", [P, CI, CH], FP32R) for i in range(2)]
        ctx_lo = [sb(f"ctx_lo{i}", [P, CI, CH], FP32R) for i in range(2)]
        kparts = sb("kparts", [P, 3, CI, CH], BF16)
        krest = sb("krest", [P, CH])
        kstack = [sb(f"kstack{i}", [P, H, CH], BF16) for i in range(2)]
        qparts = sb("qparts", [P, 3, CI, S], BF16)
        qnext, qstack = sb("qnext", [P, H, S], BF16), sb("qstack", [P, H, S], BF16)
        values = [sb(f"values{i}", [P, TT, H, 32]) for i in range(2)]
        probs = [sb(f"probs{i}", [P, GH * S]) for i in range(NPROB)]
        ksample = sb("ksample", [P, CI, H // 2, SAMPLE], BF16)
        chunk_max = sb("chunk_max", [P, ST, H, NCH])
        neg_max = sb("neg_max", [P, ST, 2, H])
        shift_hi, shift_parts = sb("shift_hi", [P, S], BF16), sb("shift_parts", [P, S], BF16)
        one_hot = sb("one_hot", [P, H], BF16)
        low_part = sb("low_part", [P, 1])
        den_in = sb("den_in", [P, 2, H])
        den_ok = sb("den_ok", [P, 2])
        verdict, verdict_int = sb("verdict", [1, 1]), sb("verdict_int", [1, 1], INT32)

        xs, xn = sb("xs", [P, ST, D]), sb("xn", [P, ST, D])
        xT = sb("xT", [P, CI, S])
        stats, mv = sb("stats", [P, ST, 6]), sb("mv", [P, ST, 2])
        veps, rstd = sb("veps", [P, ST]), sb("rstd", [P, ST])
        rden = sb("rden", [P, H])
        y = sb("y", [P, ST, D])
        qk = sb("qk", [P, ST, 2 * D])
        o_sb = qk[:, :, :].rearrange("p t (g s) -> p (t g) s", s=S)
        v1 = sb("v1", [P, ST, H, 32])
        ss, rnorm = sb("ss", [P, ST, 2 * H]), sb("rnorm", [P, ST, 2 * H])
        qkT = sb("qkT", [P, 4, S])
        feat = sb("feat", [P, 2, 2, S])
        kfeat = sb("kfeat", [P, 2, 2, S])
        amat = sb("amat", [P, GH, 3 * P])
        flat_amat = amat[:, :, :].rearrange("p a b -> p (a b)")
        wg_int = flat_amat.bitcast(INT32).rearrange("p (i n) -> p i n", i=CI)
        wu_int = [t[:, :, :, :].rearrange("p a b c -> p (a b c)")[:, 0:HID].bitcast(INT32) for t in (feat, kfeat)]
        hid = flat_amat.rearrange("p (k s) -> p k s", s=S)
        x_parts = [sb("x_hi", [P, CI, S], FP32R)[:, :, :], sb("x_lo", [P, CI, S], FP32R)[:, :, :]]
        gate_e, up = kfeat[:, 0, :, :], kfeat[:, 1, :, :]
        wstage = feat[:, :, :, :].rearrange("p a b c -> p (a b c)")

        ps_s = [ctx.enter_context(nc.psum_tensor(f"ps_s{i}", [P, 1024], FP32)) for i in range(2)]
        ps_o = ctx.enter_context(nc.psum_tensor("ps_o", [P, 1024], FP32))
        ps_p = ctx.enter_context(nc.psum_tensor("ps_p", [P, 512], FP32))
        ps_a = ctx.enter_context(nc.psum_tensor("ps_a", [P, 512], FP32))

        w_in, b_in, late_in, om_in, i_in, w_ready = (
            sem(n) for n in ("w_in", "b_in", "late_in", "om_in", "i_in", "w_ready"))
        setup_dve, setup_pool, setup_pow = sem("setup_dve"), sem("setup_pool"), sem("setup_pow")
        hot_rows = sem("hot_rows")
        judged = sem("judged")
        fast = Signals(sem, "f_", HEAD)
        general = Signals(sem, "g_", HEAD_GENERAL)

        block = ctx.enter_context(nc.Block())
        BS = NCH * STEPS

        def looped_passes(eng, body, p0=0):
            body(p0, 0, p0 // 2, True, False)
            with eng.Fori(0, NCH // 2 - 1) as c:
                body(c * 2 + (p0 + 1), 1, c + p0 // 2, False, False)
                body(c * 2 + (p0 + 2), 0, c + (p0 // 2 + 1), False, False)
            body(p0 + NCH - 1, 1, p0 // 2 + NCH // 2 - 1, False, True)

        def unrolled_passes(body):
            for p in range(NCH):
                body(p, p % 2, p // 2, p == 0, p == NCH - 1)

        def stages_at(step, table, behind=None):
            return [n for n in table if table[n] + (behind or {}).get(n, 0) == step]

        def bank_of(c, name, clock, alone):
            if not alone or name == "down":
                return ps_a
            k = c.stages["product"][clock[2]].index(name) % BANKS_ALONE
            return ps_s[k // 2][:, k % 2 * 512:(k % 2 + 1) * 512]

        def head_of(b):
            return (b, b - 1, False)

        def tail_of(b):
            return (b + 2, b, True)

        def head_general(b):
            return (b, b, False)

        def tail_general(b):
            return (b + 1, b, True)

        def wr(a):
            return a.rearrange("(i p) n -> p i n", p=P)

        @block.sync
        def _(sp):
            def reg(value):
                return value if isinstance(value, int) else sp.to_reg(value)

            def address(value):
                return value if isinstance(value, int) else sp.snap(value)

            def wait_all(*pairs):
                pairs = [(s, reg(v)) for s, v in pairs]
                for s, v in pairs:
                    sp.wait_ge(s, v)

            def load_ctx(c, ppb, q):
                b, t0 = address((q // ppb) % B), address((q % NCH) * CH)
                if not (isinstance(q, int) and q == 0):
                    wait_all((c["ctx_split"], q))
                src = ctxT.rearrange("b (i p) t -> p b i t", p=P)
                sp.dma_start(ctx_raw[:, :, :],
                             src[:, bass.ds(b, 1), :, bass.ds(t0, CH)].rearrange("p b i t -> p (b i) t")
                             ).then_inc(c["ctx_in"], 16)

            def write_keys(c, q):
                for j in range(CI):
                    wait_all((c["k_parts"], q * 2 + (j + 1)))
                    sp.dma_start(kscr[:, j * P:(j + 1) * P, :].rearrange("i p t -> p i t"),
                                 kparts[:, :, j, :]).then_inc(c["k_written"], 16)

            def stack_keys(c, q, par, used=None):
                wait_all((c["k_written"], q * 32 + 32), *([used] if used else []))
                for n in range(SLOTS):
                    sp.dma_start(kstack[par][n * DH:(n + 1) * DH, :, :],
                                 kscr[KEY_PART[n]].rearrange("(h d) t -> d h t", d=DH)
                                 ).then_inc(c["k_stacked"][par], 16)

            def load_x(c, b, *waits):
                b = address(b)
                wait_all(*waits)
                sp.dma_start(xs[:, :, :],
                             x[bass.ds(b, 1), :, :].rearrange("b (i p) d -> p (b i) d", p=P)).then_inc(c["x_in"], 16)

            def write_queries(c, clock):
                wait_all((c["operand"], c.at("operand", clock, "q")))
                sp.dma_start(qscr.rearrange("i (j p) s -> p (i j) s", p=P),
                             qparts[:, :, :, :].rearrange("p i j s -> p (i j) s")).then_inc(c["q_written"], 16)

            def stack_queries(c, heads):
                wait_all((c["q_written"], heads * 16 + 16))
                for n in range(SLOTS):
                    sp.dma_start(qnext[n * DH:(n + 1) * DH, :, :],
                                 qscr[QUERY_PART[n]].rearrange("(h d) s -> d h s", d=DH)).then_inc(c["q_stacked"], 16)

            def write_output(c, clock):
                wait_all((c["operand"], c.at("operand", clock, "oT1")))
                for t in range(ST):
                    sp.dma_start(oscr[:, t * P:(t + 1) * P, :].rearrange("h s d -> s h d"),
                                 y[:, t, :].rearrange("p (h d) -> p h d", h=H)).then_inc(c["o_written"], 16)

            def regroup_output(c, tails):
                wait_all((c["o_written"], tails * 32 + 32))
                sp.dma_start(y[:, :, :], oscr.rearrange("(t a) (u s) d -> (a u) t (s d)", t=ST, u=S // DH)
                             ).then_inc(c["o_in"], 16)

            def store(c, clock, b):
                b = address(b)
                wait_all((c["operand"], c.at("operand", clock, "down")))
                sp.dma_start(out[bass.ds(b, 1), :, :].rearrange("b (i p) d -> p (b i) d", p=P),
                             y[:, :, :]).then_inc(c["stored"], 16)

            sp.sem_inc(fast["stored"], 16)
            sp.dma_start(wstage[:, 0:CI * D].rearrange("p (i n) -> p i n", i=CI), wr(wkT)).then_inc(w_in, 16)
            sp.dma_start(wstage[:, CI * D:2 * CI * D].rearrange("p (i n) -> p i n", i=CI), wr(wvT)).then_inc(w_in, 16)
            load_ctx(fast, NCH, 0)
            load_x(fast, 0)
            sp.dma_start(bk_sb[:, :], bk).then_inc(b_in, 16)
            sp.dma_start(bq_sb[:, :], bq).then_inc(b_in, 16)
            sp.dma_start(wq_sb[:, :, :], wr(wqT)).then_inc(b_in, 16)
            sp.dma_start(bv_sb[:, :], bv.partition_broadcast(P)).then_inc(b_in, 16)
            load_ctx(fast, NCH, 1)
            write_keys(fast, 0)
            stack_keys(fast, 0, 0)
            write_queries(fast, (0, 0, False))
            stack_queries(fast, 0)

            def fast_pass(b, tail):
                def body(p, par, half, first, last):
                    q = b * NCH + p
                    steps = b * BS + p * STEPS
                    load_ctx(fast, NCH, q + 2)
                    if not tail and last:
                        load_x(fast, 1, (fast["operand"], fast.at("operand", (0, 0, False), "ln0")))
                    if first and tail:
                        load_x(fast, b - 1, (fast["operand"], fast.at("operand", head_of(b), "ln0")))
                    if tail and first:
                        write_output(fast, tail_of(b - 1))
                    write_keys(fast, q + 1)
                    if tail and first:
                        regroup_output(fast, b - 1)
                    stack_keys(fast, q + 1, 1 - par, (fast["exp_done"], steps + 2))
                    if tail and p == AT["down"] // STEPS:
                        store(fast, tail_of(b - 1), b - 1)
                        load_x(fast, (b + 1) % B, (fast["operand"], fast.at("operand", tail_of(b - 1), "down")))
                    if last:
                        write_queries(fast, (b + 1, b, False))
                        stack_queries(fast, b + 1)
                return body

            looped_passes(sp, fast_pass(0, False))
            with sp.Fori(1, B) as b:
                unrolled_passes(fast_pass(b, True))
            load_x(fast, B - 1, (fast["operand"], fast.at("operand", (B, B - 1, False), "ln0")))
            write_output(fast, tail_of(B - 1))
            regroup_output(fast, B - 1)
            store(fast, tail_of(B - 1), B - 1)
            sp.wait_ge(fast["stored"], B * 16 + 16)
            sp.wait_ge(fast["k_stacked"][0], (B * NCH // 2 + 1) * 96)
            sp.wait_ge(fast["k_stacked"][1], (B * NCH // 2) * 96)
            sp.wait_ge(fast["ctx_in"], (B * NCH + 2) * 16)
            sp.wait_ge(fast["q_stacked"], (B + 1) * 16 * SLOTS)
            sp.sem_inc(fast["landed"], 1)

            sp.wait_ge(judged, 3)
            with sp.If(sp.value_load(verdict_int[0:1, 0:1]) < 1):
                c = general
                sp.sem_inc(c["stored"], 16)
                load_ctx(c, 2 * NCH, 0)
                load_ctx(c, 2 * NCH, 1)
                write_keys(c, 0)
                stack_keys(c, 0, 0)
                with sp.Fori(0, B) as b:
                    load_x(c, b, (c["stored"], b * 16 + 16))
                    write_queries(c, head_general(b))
                    stack_queries(c, b)

                    def general_pass(attend):
                        def body(p, par, half, first, last):
                            q = b * (2 * NCH) + p
                            if attend and first:
                                used = (c["mscores"], b * BS + BS)
                            elif attend:
                                used = (c["scores"], b * BS + (p - NCH) * STEPS)
                            elif first:
                                used = (c["exp_done"], b * BS + 2)
                            else:
                                used = (c["mscores"], b * BS + p * STEPS)
                            load_ctx(c, 2 * NCH, q + 2)
                            write_keys(c, q + 1)
                            stack_keys(c, q + 1, 1 - par, used)
                        return body

                    looped_passes(sp, general_pass(False))
                    looped_passes(sp, general_pass(True), NCH)
                    load_x(c, b, (c["operand"], c.at("operand", head_general(b), "ln0")))
                    write_output(c, tail_general(b))
                    regroup_output(c, b)
                    store(c, tail_general(b), b)
                sp.wait_ge(c["stored"], B * 16 + 16)
                sp.wait_ge(c["k_stacked"][0], (B * NCH + 1) * 96)
                sp.wait_ge(c["k_stacked"][1], (B * NCH) * 96)
                sp.wait_ge(c["ctx_in"], (2 * B * NCH + 2) * 16)

        @block.tensor
        def _(pe):
            mm = nc.tensor.matmul

            def project(c, unit, q, par):
                kind, j, part = unit
                hi, lo = ctx_hi[par], ctx_lo[par]
                if kind == "k":
                    k = part
                    for n, (w, a) in enumerate(((wk[0], hi), (wk[1], hi), (wk[0], lo))):
                        last = mm(ps_p[:, :], w[:, k, j * P:(j + 1) * P], a[:, k, :],
                                  start=(k == 0 and n == 0), stop=(k == CI - 1 and n == 2))
                    if part == CI - 1:
                        last.then_inc(c["k_proj"], 1)
                else:
                    for k in range(CI):
                        for n, (a, w) in enumerate(((hi, wv[0]), (lo, wv[0]), (hi, wv[1]))):
                            last = mm(ps_p[:, 0:D], a[:, k, j * P:(j + 1) * P], w[:, k, :],
                                      start=(k == 0 and n == 0), stop=(k == CI - 1 and n == 2))
                    last.then_inc(c["v_proj"], 1)

            def project_free(c, unit, q, vt):
                kind, j, part = unit
                if kind == "k" and part == 0:
                    pe.wait_ge(c["k_out"], q * 2 + (j + 1))
                    if j == 0:
                        pe.wait_ge(c["ctx_split"], q + 1)
                        pe.wait_ge(c["v_ready"], vt + 1)
                elif kind == "v":
                    pe.wait_ge(c["v_ready"], vt + (j + 1))
                    if j == 0:
                        pe.wait_ge(c["k_out"], q * 2 + 3)

            def transpose_blocks(bank, src):
                for i in range(CI):
                    for s in range(ST):
                        last = nc.tensor.transpose(bank[:, i * S + s * P:i * S + (s + 1) * P],
                                                   src[:, s, i * P:(i + 1) * P], ident[:, :])
                return last

            def rows(bank, w, n, col=0):
                for t in range(ST):
                    for k in range(CI):
                        last = mm(bank[:, t * n:(t + 1) * n], xT[:, k, t * P:(t + 1) * P], w[:, k, col:col + n],
                                  start=k == 0, stop=k == CI - 1)
                return last

            def stage(c, name, clock, alone):
                pe.wait_ge(c["operand"], c.ready(clock, name, BANKS_ALONE if alone else 1))
                bank = bank_of(c, name, clock, alone)
                kind, n = name.rstrip("0123456789"), name[len(name.rstrip("0123456789")):]
                n = int(n) if n else 0
                if name in ("ln0T", "ln1T", "ln2T"):
                    last = transpose_blocks(bank, xn)
                elif name == "q":
                    for j in range(CI):
                        for k in range(CI):
                            last = mm(bank[:, j * S:(j + 1) * S], wq_sb[:, k, j * P:(j + 1) * P], xT[:, k, :],
                                      start=k == 0, stop=k == CI - 1)
                elif kind == "max":
                    j, t = n // ST, n % ST
                    last = mm(bank[:, :], qparts[:, 0, j, t * P:(t + 1) * P],
                              ksample[:, j, :, :].rearrange("p h k -> p (h k)"), start=True, stop=True)
                elif name == "maxT":
                    for t in range(ST):
                        last = mm(bank[STACK:P, t * P:(t + 1) * P], neg_max[:, t, :, :].rearrange("p a h -> p (a h)"),
                                  ident[:, :], start=True, stop=True, skip_group_check=True)
                elif kind in ("oT", "o2T"):
                    for g in range(G):
                        last = nc.tensor.transpose(bank[:, g * P:(g + 1) * P], o_sb[:, g, n * P:(n + 1) * P],
                                                   ident[:, :])
                elif name == "yT":
                    pe.wait_ge(c["o_in"], clock[1] * 16 + 16)
                    last = transpose_blocks(bank, y)
                elif name == "y2T":
                    last = transpose_blocks(bank, y)
                elif name == "wh":
                    last = rows(bank, wh_sb, D)
                elif name == "wout":
                    last = rows(bank, wout_sb, D)
                elif kind == "qk":
                    for k in range(CI):
                        last = mm(bank[:, :], xT[:, k, n * P:(n + 1) * P], wqkv_sb[:, k, 0:2 * D],
                                  start=k == 0, stop=k == CI - 1)
                elif name == "v":
                    last = rows(bank, wqkv_sb, D, 2 * D)
                elif kind == "qkT":
                    for i in range(4):
                        last = nc.tensor.transpose(bank[:, i * P:(i + 1) * P], qk[:, n, i * P:(i + 1) * P],
                                                   ident[:, :])
                elif kind == "feat":
                    for i in range(2):
                        last = mm(bank[:, i * S:(i + 1) * S], om_sb[:, n, :], qkT[:, 2 * i + n // 4, :],
                                  start=True, stop=True)
                elif kind == "A":
                    p = n // 2
                    pe.wait_ge(c["kfeat"], c.at("kfeat", clock, name))
                    mm(bank[:, 0:S], kfeat[:, p % 2, n % 2, 0:P], feat[:, p % 2, 0, :], start=True, stop=True)
                    last = mm(bank[:, S:S + P], kfeat[:, p % 2, n % 2, P:S], feat[:, p % 2, 0, P:S],
                              start=True, stop=True)
                elif kind == "pv":
                    for j in range(GH):
                        mm(bank[32 * j:32 * j + 32, 0:S], v1[:, 0, n * GH + j, :], amat[:, j, 0:S],
                           start=True, stop=False, skip_group_check=True)
                        last = mm(bank[32 * j:32 * j + 32, P:S], v1[:, 1, n * GH + j, :], amat[:, j, S:S + P],
                                  start=False, stop=True, skip_group_check=True)
                elif kind == "gu":
                    for i, w in enumerate((wg_r, wu_r)):
                        for k in range(CI):
                            for part in range(2):
                                last = mm(bank[:, i * S:(i + 1) * S], w[:, k, n * P:(n + 1) * P],
                                          x_parts[part][:, k, :], start=k + part == 0, stop=k + part == CI)
                elif name == "down":
                    for k in range(HB - 1 if alone else 0, HB):
                        last = down_part(c, k, bank)
                last.then_inc(c["product"], 1)

            def down_part(c, k, bank, clock=None):
                if clock is not None:
                    pe.wait_ge(c["operand"], c.at("operand", clock, f"gate{k}"))
                for t in range(ST):
                    last = mm(bank[:, t * D:(t + 1) * D], hid[:, k, t * P:(t + 1) * P], wd_sb[:, k, :],
                              start=k + t == 0, stop=k == HB - 1, skip_group_check=True)
                return last

            def products(c, names, clock, alone=False):
                for name in names:
                    if alone and name[:4] == "gate" and name != "gate0":
                        down_part(c, int(name[4:]) - 1, ps_a, clock)
                    if name not in VECTOR_ONLY:
                        stage(c, name, clock, alone)

            def value_product(c, n, s, par, starts, stops, vtile):
                i, g = s // G, s % G
                pe.wait_ge(c["exp_done"], n + 3)
                if g == 0:
                    pe.wait_ge(c["v_ready"], vtile + 2)
                for j in range(GH):
                    last = mm(ps_o[32 * j:32 * j + 32, g * S:(g + 1) * S],
                              values[par][:, i, g * GH + j, :], probs[s % NPROB][:, j * S:(j + 1) * S],
                              start=bool(starts and i == 0 and g % 2 == 0),
                              stop=bool(stops and i == TT - 1), skip_group_check=True)
                last.then_inc(c["pv_done"], 1)

            def attend_pass(c, batch, q, n0, vt, stacked, par, first, last_chunk, next_values, at_step, out_free=None):
                pe.wait_ge(c["k_stacked"][par], stacked * 96 + 96)
                for s in range(STEPS):
                    i, g = s // G, s % G
                    pe.wait_ge(c["exp_done"], n0 + (s + 1))
                    if first and s < G:
                        pe.wait_ge(c["q_ready"], batch * G + (s + 1))
                    for j in range(GH):
                        last = mm(ps_s[s % 2][:, j * S:(j + 1) * S],
                                  kstack[par][:, g * GH + j, i * P:(i + 1) * P],
                                  qstack[:, g * GH + j, :], start=True, stop=True)
                    last.then_inc(c["scores"], 1)
                    if s >= LAG:
                        if s == LAG and first and out_free is not None:
                            pe.wait_ge(c["operand"], out_free)
                        value_product(c, n0 + (s - LAG), s - LAG, par, first, last_chunk, vt + (s - LAG) // G)
                    elif not first:
                        value_product(c, n0 + (s - LAG), STEPS + s - LAG, 1 - par, False, False, vt + (-1))
                    if s in UNITS and (UNITS[s][0] == "k" or next_values):
                        project_free(c, UNITS[s], q + 1, vt + TT)
                        project(c, UNITS[s], q + 1, 1 - par)
                    at_step(s)
                if last_chunk:
                    for s in range(STEPS - LAG, STEPS):
                        value_product(c, n0 + s, s, par, False, True, vt + s // G)

            pe.sem_inc(fast["pv_done"], NPROB)
            pe.wait_ge(setup_dve, 2)
            pe.wait_ge(setup_pool, 4)
            pe.wait_ge(b_in, 16 * 4)
            for item in PROLOGUE:
                if item in HEAD:
                    products(fast, [item], (0, 0, False))
                else:
                    project_free(fast, item, 0, 0)
                    project(fast, item, 0, 0)
            pe.wait_ge(hot_rows, 2)

            def fast_pass(b, tail):
                def body(p, par, half, first, last_chunk):
                    def at_step(s):
                        if not isinstance(p, int):
                            return
                        step = p * STEPS + s
                        if tail:
                            products(fast, stages_at(step, AT), tail_of(b - 1))
                        products(fast, stages_at(step, HEAD_AT if tail else HEAD_AT_FIRST), (b + 1, b, False))

                    attend_pass(fast, b, b * NCH + p, b * BS + p * STEPS, b * (NCH * TT) + p * TT,
                                b * (NCH // 2) + half, par, first, last_chunk, True, at_step,
                                fast.at("operand", tail_of(b - 1), "o") if tail else None)
                return body

            looped_passes(pe, fast_pass(0, False))
            pe.wait_ge(late_in, 16 * 15)
            pe.wait_ge(w_ready, 1)
            with pe.Fori(1, B) as b:
                unrolled_passes(fast_pass(b, True))
            products(fast, TAIL[:NORMALISED], tail_of(B - 1), True)
            pe.wait_ge(judged, 1)
            nc.tensor.transpose(ps_a[0:1, 0:P], den_ok[:, 0:1], ident[:, :]).then_inc(judged, 1)
            products(fast, TAIL[NORMALISED:], tail_of(B - 1), True)

            pe.wait_ge(judged, 3)
            with pe.If(pe.value_load(verdict_int[0:1, 0:1]) < 1):
                pe.wait_ge(fast["landed"], 1)
                c = general
                pe.sem_inc(c["pv_done"], NPROB)
                for unit in UNITS.values():
                    if unit[0] == "k":
                        project_free(c, unit, 0, 0)
                        project(c, unit, 0, 0)
                with pe.Fori(0, B) as b:
                    products(c, ["ln0T", "q"], head_general(b))

                    def maximum_pass(p, par, half, first, last_chunk):
                        pe.wait_ge(c["k_stacked"][par], (b * NCH + half) * 96 + 96)
                        if first:
                            pe.wait_ge(c["operand"], c.at("operand", head_general(b), "qcopy0"))
                        q, n0 = b * (2 * NCH) + p, b * BS + p * STEPS
                        for s in range(STEPS):
                            t, hp = s // (H // 2), s % (H // 2)
                            pe.wait_ge(c["mreduced"], n0 + (s + 1))
                            for j in range(2):
                                h = 2 * hp + j
                                last = mm(ps_s[s % 2][:, j * CH:(j + 1) * CH],
                                          qstack[0:STACK, h, t * P:(t + 1) * P], kstack[par][0:STACK, h, :],
                                          start=True, stop=True)
                            last.then_inc(c["mscores"], 1)
                            if s in UNITS and (UNITS[s][0] == "k" or last_chunk):
                                project_free(c, UNITS[s], q + 1, b * (NCH * TT))
                                project(c, UNITS[s], q + 1, 1 - par)

                    looped_passes(pe, maximum_pass)
                    products(c, ["maxT"], head_general(b))

                    def general_attend(p, par, half, first, last_chunk):
                        attend_pass(c, b, b * (2 * NCH) + p, b * BS + (p - NCH) * STEPS,
                                    b * (NCH * TT) + (p - NCH) * TT, b * NCH + half, par, first, last_chunk,
                                    not last_chunk, lambda s: None)

                    looped_passes(pe, general_attend, NCH)
                    products(c, TAIL, tail_general(b), True)

        @block.gpsimd
        def _(pool):
            pool.memset(om_sb[:, :, :], 0.0).then_inc(setup_pool, 1)
            pool.memset(ident[:, :], 0.0)
            pool.memset(causal[:, :], 1.0)
            pool.memset(head_mask[:, :], 1.0)
            pool.memset(one_hot[:, :], 0.0)
            pool.memset(low_part[:, :], -1.0)
            pool.memset(half_power[:, :, :], -0.5)
            pool.memset(root_power[:, :], 0.5).then_inc(setup_pool, 1)
            pool.drain()
            pool.affine_select(out=ident[:, :], in_=ident[:, :], compare_op=ALU.not_equal, fill=1.0,
                               base=0, pattern=[[-1, P]], channel_multiplier=1).then_inc(setup_pool, 1)
            pool.affine_select(out=head_mask[:, :], in_=head_mask[:, :], compare_op=ALU.is_ge, fill=0.0,
                               base=0, pattern=[[-DH, H // 2]], channel_multiplier=1)
            pool.drain()
            pool.affine_select(out=head_mask[:, :], in_=head_mask[:, :], compare_op=ALU.is_ge, fill=0.0,
                               base=DH - 1, pattern=[[DH, H // 2]], channel_multiplier=-1)
            pool.affine_select(out=one_hot[:, :], in_=one_hot[:, :], compare_op=ALU.not_equal, fill=1.0,
                               base=-STACK, pattern=[[-1, H]], channel_multiplier=1)
            pool.affine_select(out=low_part[:, :], in_=low_part[:, :], compare_op=ALU.is_ge, fill=0.0,
                               base=-(STACK + H), pattern=[[0, 1]], channel_multiplier=1)
            pool.drain()
            pool.affine_select(out=one_hot[:, :], in_=one_hot[:, :], compare_op=ALU.not_equal, fill=1.0,
                               base=-(STACK + H), pattern=[[-1, H]], channel_multiplier=1)
            for k in (0, 2):
                blk = causal[:, k * P:(k + 1) * P]
                last = pool.affine_select(out=blk, in_=blk, compare_op=ALU.is_ge, fill=0.0,
                                          base=0, pattern=[[1, P]], channel_multiplier=-1)
            last.then_inc(setup_pool, 1)

            def power(c, name, clock):
                pool.wait_ge(c["variance"], c.at("powered", clock, name))
                if name[:4] == "norm":
                    n = int(name[4:])
                    pool.tensor_tensor(rnorm[:, n, :], ss[:, n, :], half_power[:, n, :], ALU.pow
                                       ).then_inc(c["powered"], 1)
                else:
                    pool.tensor_tensor(rstd[:, :], veps[:, :], half_power[:, :, 0], ALU.pow
                                       ).then_inc(c["powered"], 1)

            power(fast, "ln0", (0, 0, False))
            pool.wait_ge(fast["q_written"], 16)
            for dst, src in ((wh_sb, whT), (wout_sb, wout), (wqkv_sb, wqkv)):
                pool.dma_start(dst[:, :, :], wr(src)).then_inc(late_in, 16)
            for dst, src in ((bh_sb, bh), (bout_sb, bout), (bqkv_sb, bqkv), (node_amp, nodes)):
                pool.dma_start(dst[:, :], src.partition_broadcast(P)).then_inc(late_in, 16)
            for k in range(2 * R):
                r = k % R
                pool.dma_start(node[k * M:(k + 1) * M, :], nodes[r:r + 1].partition_broadcast(M)).then_inc(late_in, 16)
                pool.dma_start(weight[k * M:(k + 1) * M, :], weights[r:r + 1].partition_broadcast(M)).then_inc(late_in, 16)
            for h in range(H):
                row, col = (h % 8) * DH, (h % 2) * F
                pool.dma_start(om_sb[row:row + DH, h // 2, col:col + F],
                             omega[h * DH:(h + 1) * DH, :]).then_inc(om_in, 16)
            pool.dma_start(wg_int, wr(wgT)).then_inc(i_in, 16)
            for k in range(CI):
                pool.dma_start(wu_int[k], wuT[k * P:(k + 1) * P, :]).then_inc(i_in, 16)
            pool.dma_start(wd_sb[:, :, :].bitcast(INT32), wr(wdT)).then_inc(i_in, 16)

            def tail(c, clock):
                power(c, "wh", clock)
                power(c, "norm0", clock)
                power(c, "norm1", clock)
                for p in range(H // 2):
                    pool.wait_ge(c["acted"], c.at("acted", clock, f"feat{p}"))
                    for k in range(2):
                        pool.tensor_tensor(kfeat[:, p % 2, k, :], feat[:, p % 2, 1, :],
                                           half_mask[:, k:k + 1].to_broadcast([P, S]), ALU.mult
                                           ).then_inc(c["kfeat"], 1)
                power(c, "wout", clock)

            pool.wait_ge(setup_pow, 1)
            pool.tensor_tensor(node_amp[:, :], node_amp[:, :], root_power[:, :], ALU.pow).then_inc(setup_pow, 1)
            power(fast, "ln0", (1, 0, False))
            with pool.Fori(1, B) as b:
                tail(fast, tail_of(b - 1))
                power(fast, "ln0", (b + 1, b, False))
            tail(fast, tail_of(B - 1))
            pool.wait_ge(judged, 3)
            with pool.If(pool.value_load(verdict_int[0:1, 0:1]) < 1):
                pool.wait_ge(fast["landed"], 1)
                with pool.Fori(0, B) as b:
                    power(general, "ln0", head_general(b))
                    tail(general, tail_general(b))

        @block.scalar
        def _(act):
            def probabilities(c, n, s):
                act.wait_ge(c["scores"], n + 1)
                act.wait_ge(c["pv_done"], n + 1)
                nc.scalar.activation(probs[s % NPROB][:, :], ps_s[s % 2][:, :], ACT.Exp,
                                     scale=float(DH) ** -0.5).then_inc(c["exp_done"], 1)

            def stage(c, name, clock, alone=False):
                if name in FEATS:
                    p = FEATS.index(name)
                    act.wait_ge(c["operand"], c.at("operand", clock, name))
                    nc.scalar.activation(feat[:, p % 2, :, :], feat[:, p % 2, :, :], ACT.Exp, bias=node_neg[:, :]
                                         ).then_inc(c["acted"], 1)
                else:
                    k = GATES.index(name)
                    act.wait_ge(c["product"], c.at("product", clock, name))
                    bank = bank_of(c, name, clock, alone)
                    nc.scalar.activation(gate_e[:, k % 2, :], bank[:, 0:S], ACT.Exp, scale=-QUANT)
                    nc.scalar.activation(up[:, k % 2, :], bank[:, S:2 * S], ACT.Copy).then_inc(c["acted"], 1)

            def loop_of_steps(c, b):
                with act.Fori(0, 2) as half:
                    for s in range(BS // 2):
                        probabilities(c, b * BS + half * (BS // 2) + s, s % STEPS)

            act.wait_ge(setup_pool, 4)
            for i in range(2):
                nc.scalar.activation(kstack[i][STACK:P, :, :], one_hot[STACK:P, :].unsqueeze(2)
                                     .to_broadcast([P - STACK, H, CH]), ACT.Copy).then_inc(hot_rows, 1)
            act.sem_inc(fast["exp_done"], 2)
            loop_of_steps(fast, 0)
            mine = {n: AT[n] for n in FEATS + GATES}
            with act.Fori(1, B) as b:
                for step in range(BS):
                    probabilities(fast, b * BS + step, step % STEPS)
                    for name in stages_at(step, mine, ACT_BEHIND):
                        stage(fast, name, tail_of(b - 1))
            for name in FEATS + GATES:
                stage(fast, name, tail_of(B - 1), True)
            act.wait_ge(judged, 3)
            with act.If(act.value_load(verdict_int[0:1, 0:1]) < 1):
                act.wait_ge(fast["landed"], 1)
                act.sem_inc(general["exp_done"], 2)
                with act.Fori(0, B) as b:
                    loop_of_steps(general, b)
                    for name in FEATS + GATES:
                        stage(general, name, tail_general(b), True)

        @block.vector
        def _(dve):
            v = nc.vector

            def cut(hi, lo, src):
                v.tensor_copy(hi, src)
                dve.drain()
                return v.tensor_tensor(lo, src, hi.bitcast(FP32), ALU.subtract)

            def split_ctx(c, q, par):
                dve.wait_ge(c["ctx_in"], q * 16 + 16)
                cut(ctx_hi[par][:, :, :], ctx_lo[par][:, :, :], ctx_raw[:, :, :]).then_inc(c["ctx_split"], 1)

            def keys_out(c, q, j):
                dve.wait_ge(c["k_proj"], q * 2 + (j + 1))
                if j == 0 and not (isinstance(q, int) and q == 0):
                    dve.wait_ge(c["k_written"], q * 32)
                bias = bk_sb[:, j:j + 1]
                v.tensor_scalar(kparts[:, 0, j, :], ps_p[:, :], bias, None, ALU.add)
                dve.drain()
                v.scalar_tensor_tensor(krest[:, :], ps_p[:, :], bias, kparts[:, 0, j, :], ALU.add, ALU.subtract
                                       ).then_inc(c["k_out"], 1)
                dve.drain()
                v.tensor_copy(kparts[:, 1, j, :], krest[:, :])
                dve.drain()
                v.tensor_tensor(kparts[:, 2, j, :], krest[:, :], kparts[:, 1, j, :], ALU.subtract
                                ).then_inc(c["k_parts"], 1)

            def values_out(c, vt, tile, par, steps_before):
                dve.wait_ge(c["v_proj"], vt + (tile + 1))
                if tile == 0 and steps_before is not None:
                    dve.wait_ge(c["pv_done"], steps_before + NPROB)
                v.tensor_tensor(values[par][:, tile, :, 0:DH],
                                ps_p[:, 0:D].rearrange("p (h d) -> p h d", h=H),
                                bv_sb[:, :].rearrange("p (h d) -> p h d", h=H), ALU.add).then_inc(c["v_ready"], 1)

            def layernorm(c, name, clock):
                for t in range(ST):
                    v.bn_stats(stats[:, t, :], xs[:, t, :])
                dve.drain()
                for t in range(ST):
                    v.bn_aggr(mv[:, t, :], stats[:, t, :])
                dve.drain()
                v.tensor_scalar(veps[:, :], mv[:, :, 1], EPS, None, ALU.add).then_inc(c["variance"], 1)
                dve.wait_ge(c["powered"], c.at("powered", clock, name))
                for t in range(ST):
                    last = v.tensor_scalar(xn[:, t, :], xs[:, t, :], mv[:, t, 0:1], rstd[:, t:t + 1],
                                           ALU.subtract, ALU.mult)
                return last

            def normalise(bank, t, floor):
                heads = bank[:, :].rearrange("p (h c) -> p h c", c=32)
                if floor is None:
                    v.tensor_scalar(den_in[:, 0, :], heads[:, :, DH], DEN_LEAST, DEN_MOST, ALU.max, ALU.min)
                    v.reciprocal(rden[:, :], heads[:, :, DH])
                    dve.drain()
                    v.tensor_tensor(den_in[:, 1, :], den_in[:, 0, :], heads[:, :, DH], ALU.is_equal)
                    dve.drain()
                    v.tensor_reduce(den_ok[:, 1:2], den_in[:, 1, :], AX.X, ALU.min)
                    dve.drain()
                    v.tensor_tensor(den_ok[:, 0:1], den_ok[:, 0:1], den_ok[:, 1:2], ALU.min)
                else:
                    v.tensor_scalar(rden[:, :], heads[:, :, DH], floor, None, ALU.max)
                    dve.drain()
                    v.reciprocal(rden[:, :], rden[:, :])
                    dve.drain()
                return v.tensor_tensor(y[:, t, :].rearrange("p (h d) -> p h d", d=DH), heads[:, :, 0:DH],
                                       rden[:, :].unsqueeze(2).to_broadcast([P, H, DH]), ALU.mult)

            def stage(c, name, clock, alone=False, used=None):
                heads, tails, is_tail = clock
                kind, n = name.rstrip("0123456789"), name[len(name.rstrip("0123456789")):]
                n = int(n) if n else 0
                if alone or name in VECTOR_ONLY:
                    dve.drain()
                if name in ("wh", "wout"):
                    if name == "wh":
                        dve.wait_ge(c["x_in"], c.at("x_in", clock, "x") * 16)
                    v.tensor_tensor(xs[:, :, :], xs[:, :, :], (bh_sb if name == "wh" else bout_sb)[:, :].unsqueeze(1)
                                    .to_broadcast([P, ST, D]), ALU.add)
                    dve.drain()
                if name not in VECTOR_ONLY:
                    bank = bank_of(c, name, clock, alone)
                    dve.wait_ge(c["product"], c.at("product", clock, name))
                if name == "ln0":
                    dve.wait_ge(c["x_in"], c.at("x_in", clock, "x") * 16)
                    last = layernorm(c, name, clock)
                elif name == "ln2T":
                    last = cut(x_parts[0], x_parts[1], bank[:, :].rearrange("p (i s) -> p i s", i=CI))
                elif name in ("ln0T", "ln1T", "yT", "y2T"):
                    last = v.tensor_copy(xT[:, :, :], bank[:, :].rearrange("p (i s) -> p i s", i=CI))
                elif name == "q":
                    dve.wait_ge(c["stored"], tails * 16 + 16)
                    for j in range(CI):
                        src, bias = bank[:, j * S:(j + 1) * S], bq_sb[:, j:j + 1]
                        v.tensor_scalar(qparts[:, 0, j, :], src, bias, None, ALU.add)
                        dve.drain()
                        v.scalar_tensor_tensor(y[:, j, :], src, bias, qparts[:, 0, j, :], ALU.add, ALU.subtract)
                    dve.drain()
                    v.tensor_copy(qparts[:, 1, :, :], y[:, :, :])
                    dve.drain()
                    last = v.tensor_tensor(qparts[:, 2, :, :], y[:, :, :], qparts[:, 1, :, :], ALU.subtract)
                elif name == "kbd":
                    for j in range(CI):
                        last = v.tensor_tensor(ksample[:, j, :, :],
                                               kparts[:, 0, j, 0:SAMPLE].unsqueeze(1).to_broadcast([P, H // 2, SAMPLE]),
                                               head_mask[:, :].unsqueeze(2).to_broadcast([P, H // 2, SAMPLE]), ALU.mult)
                elif kind == "max":
                    j, t = n // ST, n % ST
                    last = v.tensor_reduce(neg_max[:, t, 0, j * (H // 2):(j + 1) * (H // 2)],
                                           bank[:, :].rearrange("p (h k) -> p h k", k=SAMPLE), AX.X, ALU.max,
                                           negate=True)
                    if name == "max3":
                        dve.drain()
                        last = v.tensor_copy(neg_max[:, :, 1, :], neg_max[:, :, 0, :])
                elif name == "fullmax":
                    v.tensor_reduce(neg_max[:, :, 0, :], chunk_max[:, :, :, :], AX.X, ALU.max, negate=True)
                    dve.drain()
                    last = v.tensor_copy(neg_max[:, :, 1, :], neg_max[:, :, 0, :])
                elif name == "maxT":
                    src = bank[STACK:P, 0:S]
                    v.tensor_copy(shift_hi[STACK:P, :], src)
                    dve.drain()
                    v.scalar_tensor_tensor(shift_parts[STACK:P, :], shift_hi[STACK:P, :], low_part[STACK:P, :], src,
                                           ALU.mult, ALU.add)
                    dve.drain()
                    last = v.tensor_copy(qnext[STACK:P, :, :],
                                         shift_parts[STACK:P, :].unsqueeze(1).to_broadcast([P - STACK, H, S]))
                elif name in ("qcopy", "qcopy0"):
                    dve.wait_ge(c["q_stacked"], heads * (16 * SLOTS) + 16 * SLOTS)
                    for g in range(G):
                        if used is not None:
                            dve.wait_ge(c["scores"], used - G + g + 1)
                        last = v.tensor_copy(qstack[:, g * GH:(g + 1) * GH, :], qnext[:, g * GH:(g + 1) * GH, :])
                        if name == "qcopy":
                            last.then_inc(c["q_ready"], 1)
                    if name == "qcopy":
                        dve.sem_inc(c["operand"], 1)
                        return
                elif name == "o":
                    dve.wait_ge(c["pv_done"], tails * BS + (BS + NPROB))
                    last = v.tensor_copy(o_sb[:, :, :], ps_o[:, :].rearrange("p (g s) -> p g s", g=G))
                elif kind == "oT":
                    last = normalise(bank, n, None)
                elif kind == "o2T":
                    last = normalise(bank, n, 1e-6)
                elif name in ("wh", "wout"):
                    v.tensor_tensor(xs[:, :, :], xs[:, :, :], bank[:, :].rearrange("p (t d) -> p t d", t=ST), ALU.add)
                    dve.drain()
                    last = layernorm(c, name, clock)
                elif kind == "qk":
                    last = v.tensor_tensor(qk[:, n, :], bank[:, :], bqkv_sb[:, 0:2 * D], ALU.add)
                elif name == "v":
                    for t in range(ST):
                        last = v.tensor_tensor(v1[:, t, :, 0:DH], bank[:, t * D:(t + 1) * D].rearrange("p (h d) -> p h d", h=H),
                                               bqkv_sb[:, 2 * D:3 * D].rearrange("p (h d) -> p h d", h=H), ALU.add)
                elif kind == "ss":
                    sq = feat[:, n, :, :].rearrange("p b s -> p (b s)")
                    v.tensor_tensor(sq, qk[:, n, :], qk[:, n, :], ALU.mult)
                    dve.drain()
                    v.tensor_reduce(ss[:, n, :], sq.rearrange("p (h d) -> p h d", d=DH), AX.X, ALU.add)
                    dve.drain()
                    v.tensor_scalar(ss[:, n, :], ss[:, n, :], 1e-24, None, ALU.max).then_inc(c["variance"], 1)
                    dve.sem_inc(c["operand"], 1)
                    return
                elif kind == "norm":
                    dve.wait_ge(c["powered"], c.at("powered", clock, name))
                    qk3 = qk[:, n, :].rearrange("p (h d) -> p h d", d=DH)
                    last = v.tensor_tensor(qk3, qk3, rnorm[:, n, :].unsqueeze(2).to_broadcast([P, 2 * H, DH]), ALU.mult)
                elif kind == "qkT":
                    last = v.tensor_copy(qkT[:, :, n * P:(n + 1) * P], bank[:, :].rearrange("p (i s) -> p i s", i=4))
                elif kind == "feat":
                    v.tensor_scalar(feat[:, n % 2, :, :].rearrange("p a s -> p (a s)"), bank[:, :],
                                    clip_most[:, :], clip_least[:, :], ALU.min, ALU.max).then_inc(c["operand"], 1)
                    return
                elif kind == "A":
                    last = v.tensor_tensor(amat[:, n % GH, :], bank[:, 0:3 * P], causal[:, :], ALU.mult)
                elif kind == "pv":
                    last = v.tensor_copy(o_sb[:, n, :], bank[:, 0:S])
                elif kind == "gu":
                    dve.wait_ge(c["acted"], c.at("acted", clock, name))
                    last = v.tensor_tensor(hid[:, n, :], up[:, n % 2, :], bank[:, 0:S], ALU.mult)
                elif kind == "gate":
                    e = gate_e[:, n % 2, :]
                    v.tensor_scalar(e, e, 1.0, None, ALU.add)
                    dve.drain()
                    v.reciprocal(e, e)
                    dve.drain()
                    last = v.tensor_tensor(hid[:, n, :], hid[:, n, :], e, ALU.mult)
                elif name == "down":
                    last = v.scalar_tensor_tensor(y[:, :, :], bank[:, :].rearrange("p (t d) -> p t d", t=ST),
                                                  QUANT ** 3, xs[:, :, :], ALU.mult, ALU.add)
                last.then_inc(c["operand"], 1)

            for i in range(2):
                v.memset(values[i][:, :, :, DH:32], 0.0)
            v.memset(v1[:, :, :, DH:32], 0.0)
            v.memset(half_mask[:, :], 0.0)
            v.memset(den_ok[:, 0:1], 1.0)
            dve.drain()
            for i in range(2):
                v.memset(values[i][:, :, :, DH:DH + 1], 1.0)
            v.memset(v1[:, :, :, DH:DH + 1], 1.0).then_inc(setup_dve, 1)
            dve.sem_inc(fast["k_out"], 1)
            dve.sem_inc(fast["v_ready"], 1)
            dve.wait_ge(w_in, 32)
            for n, w in enumerate((wk, wv)):
                src = wstage[:, n * CI * D:(n + 1) * CI * D].rearrange("p (i n) -> p i n", i=CI)
                cut(w[0][:, :, :], w[1][:, :, :], src)
            dve.drain()
            dve.sem_inc(setup_dve, 1)
            split_ctx(fast, 0, 0)
            dve.wait_ge(b_in, 16 * 4)
            dve.wait_ge(setup_pool, 4)
            for item in PROLOGUE:
                if item in HEAD:
                    stage(fast, item, (0, 0, False))
                elif item[0] == "v":
                    values_out(fast, 0, item[1], 0, None)
                elif item[2] == CI - 1:
                    keys_out(fast, 0, item[1])
            split_ctx(fast, 1, 1)
            stage(fast, "qcopy", (0, 0, False))

            def setup_tail():
                dve.wait_ge(late_in, 16 * 15)
                v.tensor_scalar(node_amp[:, :], node_amp[:, :], 0.0, 2.0, ALU.max, ALU.mult).then_inc(setup_pow, 1)
                v.tensor_scalar(node_neg[:, :], node[:, :], -1.0, None, ALU.mult)
                v.tensor_scalar(clip_most[:, :], node[:, :], 20.0, None, ALU.add)
                v.tensor_scalar(clip_least[:, :], node[:, :], -20.0, None, ALU.add)
                for k in range(2):
                    v.tensor_scalar(half_mask[k * F:(k + 1) * F, k:k + 1], weight[k * F:(k + 1) * F, :],
                                    0.0, 1.0 / M, ALU.max, ALU.mult)
                dve.wait_ge(setup_pow, 2)
                dve.wait_ge(om_in, 16 * H)
                om = om_sb[:, :, :].rearrange("p h (k r m) -> p (h k) r m", r=R, m=M)
                for r in range(R):
                    v.tensor_scalar(om[:, :, r, :], om[:, :, r, :], node_amp[:, r:r + 1], None, ALU.mult)
                dve.wait_ge(i_in, 16 * (CI + 2))
                v.tensor_copy(wg_r[:, :, :], wg_int)
                for k in range(CI):
                    v.tensor_copy(wu_r[:, k, :], wu_int[k])
                v.tensor_copy(wd_sb[:, :, :], wd_sb[:, :, :].bitcast(INT32))
                dve.drain()
                dve.sem_inc(w_ready, 1)

            def fast_pass(b, tail):
                def body(p, par, half, first, last_chunk):
                    q = b * NCH + p
                    if not tail and last_chunk:
                        setup_tail()
                    if tail and first:
                        stage(fast, "qcopy", head_of(b), used=b * BS)
                    for s in range(STEPS):
                        if s in UNITS:
                            kind, j, part = UNITS[s]
                            if kind == "k" and part == CI - 1:
                                keys_out(fast, q + 1, j)
                            if kind == "v":
                                values_out(fast, b * (NCH * TT) + (p + 1) * TT, j, 1 - par, b * BS + p * STEPS)
                        if s == (SPLIT_LAST if last_chunk else SPLIT):
                            split_ctx(fast, q + 2, par)
                        if isinstance(p, int):
                            if tail:
                                for name in stages_at(p * STEPS + s, AT):
                                    stage(fast, name, tail_of(b - 1))
                            for name in stages_at(p * STEPS + s, HEAD_AT if tail else HEAD_AT_FIRST):
                                stage(fast, name, (b + 1, b, False))
                return body

            looped_passes(dve, fast_pass(0, False))
            with dve.Fori(1, B) as b:
                unrolled_passes(fast_pass(b, True))
            dve.sem_inc(fast["operand"], 1)
            for name in TAIL[:NORMALISED]:
                stage(fast, name, tail_of(B - 1), True)
            dve.drain()
            dve.sem_inc(judged, 1)
            dve.wait_ge(judged, 2)
            v.tensor_reduce(verdict[:, :], ps_a[0:1, 0:P], AX.X, ALU.min)
            dve.drain()
            v.tensor_copy(verdict_int[:, :], verdict[:, :]).then_inc(judged, 1)
            for name in TAIL[NORMALISED:]:
                stage(fast, name, tail_of(B - 1), True)

            dve.wait_ge(judged, 3)
            with dve.If(dve.value_load(verdict_int[0:1, 0:1]) < 1):
                dve.wait_ge(fast["landed"], 1)
                c = general
                dve.sem_inc(c["k_out"], 1)
                dve.sem_inc(c["v_ready"], 1)
                dve.sem_inc(c["mreduced"], 2)
                split_ctx(c, 0, 0)
                for j in range(CI):
                    keys_out(c, 0, j)
                split_ctx(c, 1, 1)
                with dve.Fori(0, B) as b:
                    for name in ("ln0", "ln0T", "q", "qcopy0"):
                        stage(c, name, head_general(b))

                    def maximum_pass(p, par, half, first, last_chunk):
                        q, n0 = b * (2 * NCH) + p, b * BS + p * STEPS
                        for s in range(STEPS):
                            t, hp = s // (H // 2), s % (H // 2)
                            dve.wait_ge(c["mscores"], n0 + (s + 1))
                            v.tensor_reduce(chunk_max[:, t, 2 * hp:2 * hp + 2, bass.ds(p, 1)],
                                            ps_s[s % 2][:, :].rearrange("p (h t) -> p h t", h=2), AX.X, ALU.max
                                            ).then_inc(c["mreduced"], 1)
                            if s in UNITS:
                                kind, j, part = UNITS[s]
                                if kind == "k" and part == CI - 1:
                                    keys_out(c, q + 1, j)
                                if kind == "v" and last_chunk:
                                    values_out(c, b * (NCH * TT), j, 1 - par, b * BS)
                        split_ctx(c, q + 2, par)

                    looped_passes(dve, maximum_pass)
                    dve.drain()
                    for name in ("fullmax", "maxT", "qcopy"):
                        stage(c, name, head_general(b))

                    def general_attend(p, par, half, first, last_chunk):
                        q = b * (2 * NCH) + p
                        for j in range(CI):
                            keys_out(c, q + 1, j)
                        if not last_chunk:
                            for tile in range(TT):
                                values_out(c, b * (NCH * TT) + (p - NCH + 1) * TT, tile, 1 - par,
                                           b * BS + (p - NCH) * STEPS)
                        split_ctx(c, q + 2, par)

                    looped_passes(dve, general_attend, NCH)
                    for name in TAIL:
                        stage(c, name, tail_general(b), True)


def kernel(**inputs):
    import numpy as np
    import concourse.bacc as bacc
    from concourse.bass_utils import run_bass_kernel_spmd

    i = {k: np.asarray(a) for k, a in inputs.items()}
    omega = i["L0_attn_omega"]
    arrays = {
        "x": i["x"], "ctxT": i["ctx_1024"].transpose(0, 2, 1),
        "wqT": i["L0_xattn_Wq"].T, "bq": i["L0_xattn_bq"].reshape(CI, P).T, "wkT": i["L0_xattn_Wk"].T, "bk": i["L0_xattn_bk"].reshape(CI, P).T,
        "wvT": i["L0_xattn_Wv"].T, "bv": i["L0_xattn_bv"], "whT": i["L0_xattn_Wh"].T, "bh": i["L0_xattn_bh"],
        "wqkv": i["L0_attn_Wqkv"], "bqkv": i["L0_attn_bqkv"], "wout": i["L0_attn_Wout"], "bout": i["L0_attn_bout"],
        "omega": omega.transpose(1, 2, 0, 3).reshape(H * DH, F),
        "nodes": i["L0_attn_quad_nodes"], "weights": i["L0_attn_quad_weights"],
        "wgT": i["L0_ffn_w_gate"].T, "wuT": i["L0_ffn_w_up"].T, "wdT": i["L0_ffn_w_down"].T,
    }
    arrays = {k: np.ascontiguousarray(a) for k, a in arrays.items()}
    nc = bacc.Bacc("TRN2", target_bir_lowering=False, num_devices=1)
    aps = [nc.dram_tensor(k, a.shape, mybir.dt.from_np(a.dtype), kind="ExternalInput").ap()
           for k, a in arrays.items()]
    out = nc.dram_tensor("out", (B, S, D), FP32, kind="ExternalOutput").ap()
    perceiver(nc, *aps, out)
    r = run_bass_kernel_spmd(nc, [arrays], core_ids=[0])
    return r.results[0]["out"]
```
